# Optimizing a Trainium2 kernel written in Bass

```python
import numpy as np
import jax
import jax.numpy as jnp

def _softmax(x, axis=-1):
    return jax.nn.softmax(x, axis=axis)

def _gelu(x):
    return jax.nn.gelu(x, approximate=True)

def _silu(x):
    return jax.nn.silu(x)

def _sigmoid(x):
    return jax.nn.sigmoid(x)

def _layernorm(x, axis=-1, eps=1e-05):
    m = jnp.mean(x, axis=axis, keepdims=True)
    v = jnp.var(x, axis=axis, keepdims=True)
    return (x - m) / jnp.sqrt(v + eps)

def _scatter_add(tgt, idx, src, axis=0):
    return tgt.at[idx].add(src)

def _segment_sum(src, seg, n):
    return jax.ops.segment_sum(src, seg, n)
kernel_name = 'mk_flamingo_gated_d2_seqx_r4_942aef'

def setup_inputs(seed: int=0):
    np.random.seed(seed)
    _w = jnp.asarray

    def _rec_inputs():
        import jax
        import jax.numpy as jnp
        _rk = jax.random.key(seed)
        x = -0.0002928 + 1 * jax.random.normal(jax.random.fold_in(_rk, 1), (64, 128, 256), jnp.float32)
        _lenS = 128 - jax.random.randint(jax.random.fold_in(_rk, 7), (64,), 0, max(1, 128 // 4) + 1, jnp.int32)
        _lenS2 = 128 - jax.random.randint(jax.random.fold_in(_rk, 8), (64,), 0, max(1, 128 // 4) + 1, jnp.int32)
        _ctx_1024P = jax.random.normal(jax.random.fold_in(_rk, 11), (64, 16, 256), jnp.float32)
        _ctx_1024c = jax.random.dirichlet(jax.random.fold_in(_rk, 511), 0.3 * jnp.ones((16,), jnp.float32), (64, 128))
        _ctx_1024t = jnp.einsum('bsk,bkd->bsd', _ctx_1024c, _ctx_1024P)
        _ctx_1024t = _ctx_1024t * jax.lax.rsqrt(jnp.mean(jnp.square(_ctx_1024t)) + 1e-12) * 0.953939
        ctx_1024 = 2.81802e-05 + 1.00001 * (_ctx_1024t + 0.3 * jax.random.normal(jax.random.fold_in(_rk, 611), (64, 128, 256), jnp.float32))
        _g = jax.random.normal(jax.random.fold_in(_rk, 9001), (2, 2), jnp.float32)
        _g = jnp.sign(_g) * jnp.maximum(jnp.abs(_g), 1.0) + (_g == 0) * 1.0
        g_xattn = _g[0]
        g_ffn = _g[1]
        return (x, ctx_1024, g_xattn, g_ffn)
    x, ctx_1024, g_xattn, g_ffn = _rec_inputs()

    def _L0_xattn_setup():
        import jax, jax.numpy as jnp
        import numpy as np
        DIM = 256
        NUM_HEADS = 16
        HEAD_DIM = DIM // NUM_HEADS
        SCALE = HEAD_DIM ** (-0.5)
        key = jax.random.key(seed)
        k1, k2, k3, k4 = jax.random.split(key, 4)
        B, N_q, N_kv = (4, 256, 1024)
        q = jax.random.normal(k1, (B, N_q, DIM), dtype=jnp.float32)
        kv = jax.random.normal(k2, (B, N_kv, DIM), dtype=jnp.float32)
        W_qkv = jax.random.normal(k3, (DIM, 3 * DIM), dtype=jnp.float32) * DIM ** (-0.5)
        W_proj = jax.random.normal(k4, (DIM, DIM), dtype=jnp.float32) * DIM ** (-0.5)
        b_proj = jnp.zeros((DIM,), dtype=jnp.float32)
        return {'q': q, 'kv': kv, 'W_qkv': W_qkv, 'W_proj': W_proj, 'b_proj': b_proj}
    _L0_xattn_all = _L0_xattn_setup()
    _L0_xattn_in = {k: v for k, v in _L0_xattn_all.items() if k in ('W_qkv', 'W_proj', 'b_proj')}
    del _L0_xattn_all

    def _L0_ffn_setup():
        import math
        import jax, jax.numpy as jnp
        import numpy as np
        NUM_EXPERTS = 8
        CAPACITY_FACTOR = 1.5
        key = jax.random.key(seed)
        ks = jax.random.split(key, 4)
        B, T, D, F, E = (4, 512, 256, 1024, NUM_EXPERTS)
        scale = 0.02
        return {'x': jax.random.normal(ks[0], (B, T, D), dtype=jnp.float32), 'router_w': jax.random.normal(ks[1], (E, D), dtype=jnp.float32) * scale, 'w1': jax.random.normal(ks[2], (E, D, F), dtype=jnp.float32) * scale, 'b1': jnp.zeros((E, F), dtype=jnp.float32), 'w2': jax.random.normal(ks[3], (E, F, D), dtype=jnp.float32) * scale, 'b2': jnp.zeros((E, D), dtype=jnp.float32)}
    _L0_ffn_all = _L0_ffn_setup()
    _L0_ffn_in = {k: v for k, v in _L0_ffn_all.items() if k in ('router_w', 'w1', 'b1', 'w2', 'b2')}
    del _L0_ffn_all

    def _L1_xattn_setup():
        import jax, jax.numpy as jnp
        import numpy as np
        D_MODEL = 256
        N_HEADS = 16
        D_K = D_MODEL // N_HEADS
        key = jax.random.key(seed)
        ks = jax.random.split(key, 7)
        B, S, D = (4, 512, D_MODEL)
        scale = 1.0 / np.sqrt(D)
        return {'q': jax.random.normal(ks[0], (B, S, D), dtype=jnp.float32), 'k': jax.random.normal(ks[1], (B, S, D), dtype=jnp.float32), 'v': jax.random.normal(ks[2], (B, S, D), dtype=jnp.float32), 'wq': jax.random.normal(ks[3], (D, D), dtype=jnp.float32) * scale, 'wk': jax.random.normal(ks[4], (D, D), dtype=jnp.float32) * scale, 'wv': jax.random.normal(ks[5], (D, D), dtype=jnp.float32) * scale, 'wo': jax.random.normal(ks[6], (D, D), dtype=jnp.float32) * scale}
    _L1_xattn_all = _L1_xattn_setup()
    _L1_xattn_in = {k: v for k, v in _L1_xattn_all.items() if k in ('wq', 'wk', 'wv', 'wo')}
    del _L1_xattn_all

    def _L1_ffn_setup():
        import jax, jax.numpy as jnp
        import numpy as np
        LN_EPS = 1e-05

        def _layernorm(x, g, b):
            m = jnp.mean(x, axis=-1, keepdims=True)
            v = jnp.mean(jnp.square(x - m), axis=-1, keepdims=True)
            return (x - m) * jax.lax.rsqrt(v + LN_EPS) * g + b
        K_TOP = 2
        key = jax.random.key(seed)
        ks = jax.random.split(key, 4)
        B, N, D, E = (8, 512, 256, 4)
        s = 0.02
        return {'x': jax.random.normal(ks[0], (B, N, D), dtype=jnp.float32), 'gate_W': jax.random.normal(ks[1], (D, E), dtype=jnp.float32) * s, 'gate_b': jnp.zeros((E,), jnp.float32), 'W1': jax.random.normal(ks[2], (E, D, D), dtype=jnp.float32) * s, 'b1': jnp.zeros((E, D), jnp.float32), 'g1': jnp.ones((E, D), jnp.float32), 'be1': jnp.zeros((E, D), jnp.float32), 'W2': jax.random.normal(ks[3], (E, D, D), dtype=jnp.float32) * s, 'b2': jnp.zeros((E, D), jnp.float32), 'g2': jnp.ones((E, D), jnp.float32), 'be2': jnp.zeros((E, D), jnp.float32)}
    _L1_ffn_all = _L1_ffn_setup()
    _L1_ffn_in = {k: v for k, v in _L1_ffn_all.items() if k in ('gate_W', 'gate_b', 'W1', 'b1', 'g1', 'be1', 'W2', 'b2', 'g2', 'be2')}
    del _L1_ffn_all
    return {'x': x, 'ctx_1024': ctx_1024, 'g_xattn': g_xattn, 'g_ffn': g_ffn, 'L0_xattn_W_qkv': _L0_xattn_in['W_qkv'], 'L0_xattn_W_proj': _L0_xattn_in['W_proj'], 'L0_xattn_b_proj': _L0_xattn_in['b_proj'], 'L0_ffn_router_w': _L0_ffn_in['router_w'], 'L0_ffn_w1': _L0_ffn_in['w1'], 'L0_ffn_b1': _L0_ffn_in['b1'], 'L0_ffn_w2': _L0_ffn_in['w2'], 'L0_ffn_b2': _L0_ffn_in['b2'], 'L1_xattn_wq': _L1_xattn_in['wq'], 'L1_xattn_wk': _L1_xattn_in['wk'], 'L1_xattn_wv': _L1_xattn_in['wv'], 'L1_xattn_wo': _L1_xattn_in['wo'], 'L1_ffn_gate_W': _L1_ffn_in['gate_W'], 'L1_ffn_gate_b': _L1_ffn_in['gate_b'], 'L1_ffn_W1': _L1_ffn_in['W1'], 'L1_ffn_b1': _L1_ffn_in['b1'], 'L1_ffn_g1': _L1_ffn_in['g1'], 'L1_ffn_be1': _L1_ffn_in['be1'], 'L1_ffn_W2': _L1_ffn_in['W2'], 'L1_ffn_b2': _L1_ffn_in['b2'], 'L1_ffn_g2': _L1_ffn_in['g2'], 'L1_ffn_be2': _L1_ffn_in['be2']}

def reference(x, ctx_1024, g_xattn, g_ffn, L0_xattn_W_qkv, L0_xattn_W_proj, L0_xattn_b_proj, L0_ffn_router_w, L0_ffn_w1, L0_ffn_b1, L0_ffn_w2, L0_ffn_b2, L1_xattn_wq, L1_xattn_wk, L1_xattn_wv, L1_xattn_wo, L1_ffn_gate_W, L1_ffn_gate_b, L1_ffn_W1, L1_ffn_b1, L1_ffn_g1, L1_ffn_be1, L1_ffn_W2, L1_ffn_b2, L1_ffn_g2, L1_ffn_be2):
    import jax
    import jax.numpy as jnp

    def _L0_xattn_ref(q, kv, W_qkv, W_proj, b_proj):
        import jax, jax.numpy as jnp
        import numpy as np
        DIM = 256
        NUM_HEADS = 16
        HEAD_DIM = DIM // NUM_HEADS
        SCALE = HEAD_DIM ** (-0.5)
        B, N_q, C = q.shape
        N_kv = kv.shape[1]
        H, hd = (NUM_HEADS, HEAD_DIM)
        kv_qkv = (kv @ W_qkv).reshape(B, N_kv, 3, H, hd)
        k = jnp.transpose(kv_qkv[:, :, 1], (0, 2, 1, 3))
        v = jnp.transpose(kv_qkv[:, :, 2], (0, 2, 1, 3))
        q_qkv = (q @ W_qkv).reshape(B, N_q, 3, H, hd)
        qh = jnp.transpose(q_qkv[:, :, 0], (0, 2, 1, 3))
        attn = jnp.einsum('bhqd,bhkd->bhqk', qh, k) * SCALE
        attn = jax.nn.softmax(attn, axis=-1)
        x = jnp.einsum('bhqk,bhkd->bhqd', attn, v)
        x = jnp.transpose(x, (0, 2, 1, 3)).reshape(B, N_q, C)
        return x @ W_proj + b_proj

    def _L0_ffn_ref(x, router_w, w1, b1, w2, b2):
        import math
        import jax, jax.numpy as jnp
        import numpy as np
        NUM_EXPERTS = 8
        CAPACITY_FACTOR = 1.5
        B, T, D = x.shape
        E = router_w.shape[0]
        N = B * T
        C = max(math.ceil(CAPACITY_FACTOR * N / E), 1)
        x_flat = x.reshape(N, D)
        logits = x_flat @ router_w.T
        probs = jax.nn.softmax(logits, axis=-1)
        chosen_e = jnp.argmax(probs, axis=-1)
        chosen_p = jnp.max(probs, axis=-1)
        onehot = jax.nn.one_hot(chosen_e, E, dtype=jnp.float32)
        pos = jnp.take_along_axis(jnp.cumsum(onehot, axis=0), chosen_e[:, None], axis=1)[:, 0] - 1.0
        pos = pos.astype(jnp.int32)
        kept = pos < C
        pos_c = jnp.clip(pos, 0, C - 1)
        buf = jnp.zeros((E, C, D), dtype=x.dtype).at[chosen_e, pos_c].add(x_flat * kept[:, None].astype(x.dtype))
        h = jax.nn.gelu(jnp.einsum('ecd,edf->ecf', buf, w1) + b1[:, None, :], approximate=False)
        eo = jnp.einsum('ecf,efd->ecd', h, w2) + b2[:, None, :]
        y = eo[chosen_e, pos_c] * (chosen_p * kept.astype(x.dtype))[:, None]
        return y.reshape(B, T, D)

    def _L1_xattn_ref(q, k, v, wq, wk, wv, wo):
        import jax, jax.numpy as jnp
        import numpy as np
        D_MODEL = 256
        N_HEADS = 16
        D_K = D_MODEL // N_HEADS
        B, S, D = q.shape
        H, dk = (N_HEADS, D_K)
        qp = (q @ wq.T).reshape(B, S, H, dk).transpose(0, 2, 1, 3)
        kp = (k @ wk.T).reshape(B, S, H, dk).transpose(0, 2, 1, 3)
        vp = (v @ wv.T).reshape(B, S, H, dk).transpose(0, 2, 1, 3)
        scores = jnp.einsum('bhqd,bhkd->bhqk', qp, kp) / jnp.sqrt(jnp.float32(dk))
        attn = jax.nn.softmax(scores, axis=-1)
        out = jnp.einsum('bhqk,bhkd->bhqd', attn, vp)
        out = out.transpose(0, 2, 1, 3).reshape(B, S, D)
        return out @ wo.T

    def _L1_ffn_ref(x, gate_W, gate_b, W1, b1, g1, be1, W2, b2, g2, be2):
        import jax, jax.numpy as jnp
        import numpy as np
        LN_EPS = 1e-05

        def _layernorm(x, g, b):
            m = jnp.mean(x, axis=-1, keepdims=True)
            v = jnp.mean(jnp.square(x - m), axis=-1, keepdims=True)
            return (x - m) * jax.lax.rsqrt(v + LN_EPS) * g + b
        K_TOP = 2
        B, N, D = x.shape
        BN = B * N
        xf = x.reshape(BN, D)
        gate_scores = xf @ gate_W + gate_b
        topk_scores, topk_idx = jax.lax.top_k(gate_scores, K_TOP)
        weights = jax.nn.softmax(topk_scores, axis=-1)

        def expert(w1, bb1, gg1, bbe1, w2, bb2, gg2, bbe2):
            h = jax.nn.relu(_layernorm(xf @ w1 + bb1, gg1, bbe1))
            return _layernorm(h @ w2 + bb2, gg2, bbe2)
        all_out = jax.vmap(expert)(W1, b1, g1, be1, W2, b2, g2, be2)
        exp_out = all_out[topk_idx, jnp.arange(BN)[:, None]]
        out = jnp.sum(weights[..., None] * exp_out, axis=1)
        return (out + xf).reshape(B, N, D)
    x = x + jnp.tanh(g_xattn[0]) * _L0_xattn_ref(_layernorm(x, axis=-1), ctx_1024, L0_xattn_W_qkv, L0_xattn_W_proj, L0_xattn_b_proj)
    x = x + jnp.tanh(g_ffn[0]) * _L0_ffn_ref(_layernorm(x, axis=-1), L0_ffn_router_w, L0_ffn_w1, L0_ffn_b1, L0_ffn_w2, L0_ffn_b2)
    x = x + jnp.tanh(g_xattn[1]) * _L1_xattn_ref(_layernorm(x, axis=-1), ctx_1024, ctx_1024, L1_xattn_wq, L1_xattn_wk, L1_xattn_wv, L1_xattn_wo)
    x = x + jnp.tanh(g_ffn[1]) * _L1_ffn_ref(_layernorm(x, axis=-1), L1_ffn_gate_W, L1_ffn_gate_b, L1_ffn_W1, L1_ffn_b1, L1_ffn_g1, L1_ffn_be1, L1_ffn_W2, L1_ffn_b2, L1_ffn_g2, L1_ffn_be2)
    return x

_drawn_inputs = setup_inputs


def setup_inputs(seed=0):
    import zlib

    import numpy as np

    out = dict(_drawn_inputs(seed))
    spreads = {'g_ffn': (-1.0, 0.2),
     'L0_xattn_b_proj': (0.0, 0.1),
     'L0_ffn_b1': (0.0, 0.1),
     'L0_ffn_b2': (0.0, 0.1),
     'L1_ffn_gate_b': (0.0, 0.1),
     'L1_ffn_b1': (0.0, 0.1),
     'L1_ffn_g1': (1.0, 0.2),
     'L1_ffn_be1': (0.0, 0.1),
     'L1_ffn_b2': (0.0, 0.1),
     'L1_ffn_g2': (1.0, 0.2),
     'L1_ffn_be2': (0.0, 0.1)}
    factors = {}
    for name, (base, spread) in spreads.items():
        noise = np.random.default_rng([zlib.crc32(name.encode()), seed]).standard_normal(out[name].shape)
        drawn = base * np.exp(spread * noise) if base else spread * noise
        out[name] = jnp.asarray(drawn.astype(out[name].dtype))
    for name, factor in factors.items():
        out[name] = (out[name] * factor).astype(out[name].dtype)
    return out
```

```python
from contextlib import ExitStack

import concourse.bass as bass
from concourse import mybir

P = 128
ALU = mybir.AluOpType
ACT = mybir.ActivationFunctionType
AX_X = mybir.AxisListType.X
F32 = mybir.dt.float32
F32R = mybir.dt.float32r
BF16 = mybir.dt.bfloat16
I32 = mybir.dt.int32
U32 = mybir.dt.uint32
LN_EPS = 1e-5


class At:

    def __init__(self, pair, off, span=2):
        if isinstance(pair, int):
            pair, off = 0, span * pair + off
        self.pair, self.off, self.span = pair, off, span

    def __add__(self, n):
        return At(self.pair, self.off + n, self.span)

    def __sub__(self, n):
        return At(self.pair, self.off - n, self.span)

    @property
    def known(self):
        return isinstance(self.pair, int)

    @property
    def begun(self):
        return not self.known or self.off >= 0

    @property
    def at_edge(self):
        return self.known and self.off >= 0

    @property
    def parity(self):
        return self.off % 2

    def times(self, n, plus=0):
        return self.pair * (self.span * n) + (self.off * n + plus)

    def half(self, n, plus=0):
        return self.pair * (self.span // 2 * n) + ((self.off // 2) * n + plus)

    def within(self, count):
        return not self.known or 0 <= self.off < count


class Signal:

    def __init__(self, sem, per=1, base=0):
        self.sem, self.per, self.base = sem, per, base

    def after(self, batches):
        return Signal(self.sem, self.per, self.base + batches * self.per)

    def of(self, b):
        return self.sem

    def at(self, b, nth=None):
        return b.times(self.per, self.base + (self.per if nth is None else nth))


class Arrival:

    def __init__(self, sems, per=1, base=0):
        self.sems, self.per, self.base = sems, per, base

    def after(self, batches):
        return Arrival(self.sems, self.per, self.base + batches // 2 * 16 * self.per)

    def of(self, b):
        return self.sems[b.parity]

    def at(self, b):
        return b.half(16 * self.per, self.base + 16 * self.per)


def run_steps(eng, count, lead, tail, warm, step, span=2):
    first = -(-warm // span) * span
    last = (count - lead) // span * span
    for s in range(-lead, first):
        step(At(0, s, span))
    with eng.Fori(first // span, last // span) as turn:
        for n in range(span):
            step(At(turn, n, span))
    for s in range(last, count + tail):
        step(At(0, s, span))


def run_experts(eng, experts, step):
    def pair_of_experts(pair, e_off, g_off):
        for e in range(2):
            for t in range(3):
                step(At(pair, e_off + e), At(pair, g_off + 3 * e + t, 6), t)

    pair_of_experts(0, 0, 0)
    if experts > 4:
        with eng.Fori(1, experts // 2 - 1) as pair:
            pair_of_experts(pair, 0, 0)
    pair_of_experts(0, experts - 2, 3 * (experts - 2))


def flamingo_gated(nc, x, ctx_in, consts, gates, wq, wk, wv, wp, b_proj, router, w1_0, b1_0, w2_0, b2_0,
                   gate_w, gate_b, w1_1, b12_1, g1_1, be1_1, w2_1, g2_1, be2_1, out):
    B, S, D = x.shape
    C = D // P
    H = 16
    DH = D // H
    N = B * S
    E0 = w1_0.shape[0]
    F0 = b1_0.shape[2] * P
    FC = F0 // P
    CAP = -(-3 * N // (2 * E0))
    G = CAP // 3
    GT = G // P
    NG = 3
    E1 = w1_1.shape[1]
    SOFT = float(DH) ** -0.5
    HP = 4
    FAR = float(1 << 20)
    assert S == P and C == 2 and DH == 16 and CAP % (3 * P) == 0 and B % 2 == 0
    LEAD, TAIL, WARM = 2, 5, 6
    ATTENTION_WORDS = 15360
    ZERO_PARTS = 12
    assert E0 * CAP // P % ZERO_PARTS == 0

    es = ExitStack()
    with es:
        def sb(name, shape, dt=F32):
            return es.enter_context(nc.sbuf_tensor(name, shape, dt))

        def sem(name):
            return es.enter_context(nc.semaphore(name))

        def signal(name, per=1):
            return Signal(sem(name), per)

        def arrival(name, per=1):
            return Arrival([sem(name + "_even"), sem(name + "_odd")], per)

        x1_d = nc.dram_tensor("x1_d", (B, S, D), F32, kind="Internal").ap()
        x2_d = nc.dram_tensor("x2_d", (B, S, D), F32, kind="Internal").ap()
        x3_d = nc.dram_tensor("x3_d", (B, S, D), F32, kind="Internal").ap()
        slots_d = nc.dram_tensor("slots_d", (E0 * CAP, D), F32, kind="Internal").ap()
        eo_d = nc.dram_tensor("eo_d", (E0 * CAP, D), F32, kind="Internal").ap()
        slot_of_d = nc.dram_tensor("slot_of_d", (B, S, 1), I32, kind="Internal").ap()
        weight_of_d = nc.dram_tensor("weight_of_d", (B, S, 1), F32, kind="Internal").ap()

        ps = es.enter_context(nc.psum_tensor("ps", [P, 8, 512], F32))
        scores = ps[:, 0:4, :]
        b4, b5, b6, b7 = (ps[:, n, :] for n in (4, 5, 6, 7))

        cst = sb("cst", [P, consts.shape[1]])
        ident = cst[:, 0:128]
        head_mask = cst[:, 128:130]
        row_mask = cst[0:H, 130:134]
        iota_e = cst[:, 134:134 + E0]
        quad_rows = cst[:, 142:146]
        tri_f = cst[:, 146:274]
        hilo_mask = cst[0:2, 274:276]
        neg_half = cst[:, 276:277]
        eps = cst[:, 277:278]
        quad_ones = sb("quad_ones", [P, 4, P], F32R)
        tri = sb("tri", [P, P], BF16)
        ones_bf = sb("ones_bf", [P, P], BF16)
        g_in = sb("g_in", [P, 4])
        g_t = sb("g_t", [P, 4])
        zeros = sb("zeros", [P, D])
        pool_tick = sb("pool_tick", [1, 1])
        dve_tick = sb("dve_tick", [1, 1])

        v_aug = sb("v_aug", [P, 2, H, 32])
        nmax_x = sb("nmax_x", [P, 2, 4, P], F32R)
        base = sb("base", [P, E0])

        w_q = sb("w_q", [P, C, D])
        w_k = sb("w_k", [P, C, D])
        w_v = sb("w_v", [P, C, D])
        w_p = sb("w_p", [P, C, D])
        bp_g = sb("bp_g", [P, D])
        w_r = sb("w_r", [P, C, E0])

        phase = es.enter_context(ExitStack())

        def psb(name, shape, dt=F32):
            return phase.enter_context(nc.sbuf_tensor(name, shape, dt))

        x_in = psb("x_in", [P, 2, D])
        c_in = psb("c_in", [P, 2, D])
        y_in = psb("y_in", [P, 2, D])
        slot_in = psb("slot_in", [P, 2, 1], I32)
        weight_in = psb("weight_in", [P, 2, 1])
        x2 = psb("x2", [P, 2, D])
        st1 = psb("st1", [P, 6])
        mv1 = psb("mv1", [P, 2])
        rs1 = psb("rs1", [P, 2])
        xh = psb("xh", [P, 2, D])
        in_t = psb("in_t", [P, 2, 4, P])
        qk_hi = psb("qk_hi", [P, 2, 4, P], F32R)
        qk_lo = psb("qk_lo", [P, 2, 4, P], F32R)
        qm_hi = psb("qm_hi", [P, 2, 2, 2, P], F32R)
        qm_lo = psb("qm_lo", [P, 2, 2, 2, P], F32R)
        km_hi = psb("km_hi", [P, 2, 2, 2, P], F32R)
        nmax = psb("nmax", [P, 2, H])
        prob_t = psb("prob_t", [P, H, P])
        o_pad = psb("o_pad", [P, 4, P])
        rden = psb("rden", [P, H])
        o_n = psb("o_n", [P, 2, H, DH])
        o_t = psb("o_t", [P, 2, C, P])
        x_res = psb("x_res", [P, 2, D])
        x1 = psb("x1", [P, 2, D])
        st2 = psb("st2", [P, 6])
        mv2 = psb("mv2", [P, 2])
        rs2 = psb("rs2", [P, 2])
        xh2 = psb("xh2", [P, 4, D])
        x2_t = psb("x2_t", [P, 2, C, P])
        lg = psb("lg", [P, 2, E0])
        top = psb("top", [P, 8])
        topi = psb("topi", [P, 8], U32)
        ntop = psb("ntop", [P, 2, 1])
        ex8 = psb("ex8", [P, E0])
        den8 = psb("den8", [P, 2, 1])
        ei = psb("ei", [P, 2, 1])
        onehot = psb("onehot", [P, 2, E0], BF16)
        cum = psb("cum", [P, E0])
        cumsel = psb("cumsel", [P, E0])
        pos = psb("pos", [P, 1])
        kept = psb("kept", [P, 1])
        posc = psb("posc", [P, 1])
        far = psb("far", [P, 1])
        p8 = psb("p8", [P, 1])
        slot_f = psb("slot_f", [P, 1])
        slot_g = psb("slot_g", [P, 2, 1], I32)
        slot_s = psb("slot_s", [P, 2, 1], I32)
        wgt = psb("wgt", [P, 2, 1])

        phase.close()

        xg = psb("xg", [P, 2, GT, D])
        xgt_hi = psb("xgt_hi", [P, 2, C, G], F32R)
        xgt_lo = psb("xgt_lo", [P, 2, C, G], F32R)
        hid = psb("hid", [P, 2, G])
        hid_hi = psb("hid_hi", [P, FC, G], F32R)
        hid_lo = psb("hid_lo", [P, FC, G], F32R)
        taken = 2 * GT * D + 4 * C * G + 2 * G + 2 * FC * G
        if taken < ATTENTION_WORDS:
            psb("gap0", [P, ATTENTION_WORDS - taken])
        eo = psb("eo", [P, 2, GT, D])
        w_hi = psb("w_hi", [P, 2, 4096], F32R)
        w_lo = psb("w_lo", [P, 2, 4096], F32R)
        w_raw = psb("w_raw", [P, 4096])
        b1_in = psb("b1_in", [P, 2, FC])
        b2_in = psb("b2_in", [P, 2, D])
        phase.close()

        x3 = psb("x3", [P, 4, D])
        fst = psb("fst", [P, 6])
        fmv = psb("fmv", [P, 2])
        frs = psb("frs", [P, 2])
        xf = psb("xf", [P, 4, D])
        xft_hi = psb("xft_hi", [P, 2, C, P], F32R)
        xft_lo = psb("xft_lo", [P, 2, C, P], F32R)
        gpad = psb("gpad", [P, 2, 8])
        gtop = psb("gtop", [P, 8])
        gtopi = psb("gtopi", [P, 8], U32)
        gidx = psb("gidx", [P, 2])
        gdiff = psb("gdiff", [P, 1])
        gexp = psb("gexp", [P, 1])
        gsum = psb("gsum", [P, 1])
        gw = psb("gw", [P, 2])
        gwa = psb("gwa", [P, E1])
        gwb = psb("gwb", [P, E1])
        gwt = psb("gwt", [P, 2, E1])
        gwt_t = psb("gwt_t", [E1, 2, P])
        h_st = psb("h_st", [P, E1, 6])
        h_mv = psb("h_mv", [P, E1, 2])
        h_rs = psb("h_rs", [P, 2, E1])
        h_nm = psb("h_nm", [P, E1])
        z1 = psb("z1", [P, 2, E1, D])
        a_t = psb("a_t", [P, 2, E1, C, P])
        k_st = psb("k_st", [P, E1, 6])
        k_mv = psb("k_mv", [P, E1, 2])
        k_rs = psb("k_rs", [P, 2, E1])
        k_rw = psb("k_rw", [P, E1])
        k_nm = psb("k_nm", [P, E1])
        u2 = psb("u2", [P, 2, E1, D])
        u2g = psb("u2g", [P, E1, D])
        u2s = psb("u2s", [P, 2, D])
        u2t = psb("u2t", [P, D])
        mix1 = psb("mix1", [P, 4, D])
        mix2 = psb("mix2", [P, D])
        be_sb = psb("be_sb", [P, 2, D])
        x4 = psb("x4", [P, 2, D])
        psb("gap1", [P, 2048])
        w1f = psb("w1f", [P, E1, C, D])
        w1_hi = psb("w1_hi", [P, E1, C, D], F32R)
        w1_lo = psb("w1_lo", [P, E1, C, D], F32R)
        w2f = psb("w2f", [P, E1, C, D])
        gw_in = psb("gw_in", [P, C, E1])
        gw_hi = psb("gw_hi", [P, C, E1], F32R)
        gw_lo = psb("gw_lo", [P, C, E1], F32R)
        gb_in = psb("gb_in", [P, E1])
        b12_in = psb("b12_in", [2, 2, E1, D])
        b12_hi = psb("b12_hi", [2, 2, E1, D], F32R)
        b12_lo = psb("b12_lo", [2, 2, E1, D])
        b12 = psb("b12", [2, 2, E1, D], F32R)
        ones2 = psb("ones2", [2, P], F32R)
        g1_in = psb("g1_in", [P, E1, C])
        be1_in = psb("be1_in", [P, E1, C])
        g2_in = psb("g2_in", [P, E1, D])
        be2_in = psb("be2_in", [E1, D])

        s_set = sem("s_set")
        s_cst = sem("s_cst")
        s_cst2 = sem("s_cst2")
        s_tanh = sem("s_tanh")
        s_zeroed = sem("s_zeroed")
        s_zero_tile = sem("s_zero_tile")
        s_bp = sem("s_bp")
        s_wp = [sem(f"s_wp{n}") for n in range(2)]
        s_w = [sem(f"s_w{n}") for n in range(2)]
        s_bias = sem("s_bias")
        s_vz = sem("s_vz")

        def signals(prefix, arrivals, counts):
            named = {name: arrival(prefix + name, per) for name, per in arrivals.items()}
            named.update({name: signal(prefix + name, per) for name, per in counts.items()})
            return named

        attention = signals(
            "", dict(x_came=1, c_came=1, y_came=1, r_came=1, route_came=2, x2_stored=1, x1_stored=1, route_stored=2, scattered=1),
            dict(x2_done=1, n1_stats=2, n1_rstd=2, xh_done=1, in_turned=1, in_t_done=1, qk_done=1, qk_hi_done=1, qk_lo_done=1,
                 masked=3, v_done=1, v_out=1, s1_done=1, max_done=2, max_turned=1, nmax_done=1, s2_done=2, exp_done=2,
                 av_done=1, o_pad_done=1, o1_done=1, o_norm=2, o2_done=1, o_t_done=1, pr_done=1, res_biased=1, x1_done=1,
                 n2_stats=2, n2_rstd=2, xh2_done=1, x2_turned=1, x2_t_done=1, lg_done=1, lg_read=1, top_done=5, den_done=1,
                 cum_done=1, cum_read=1, slots_steps=10))
        only_second = ("x2_done", "y_came", "route_came", "x2_stored")
        y0 = attention
        y1 = {k: v if k in only_second else v.after(B) for k, v in attention.items()}
        sy = [y0, y1]

        z = signals(
            "z_", dict(xg_came=1, eo_stored=1),
            dict(w_came=64, wh_done=1, wl_done=1, g_turned=C, xg_hi_done=C, xg_lo_done=C, up_done=FC, hid_done=FC,
                 hid_hi_done=FC, hid_lo_done=FC, down_done=1, eo_done=GT))

        f = signals(
            "f_", dict(x3_came=1, x4_stored=1),
            dict(st=2, rstd=2, xf_done=1, x_turned=1, x_hi_done=1, x_lo_done=1, gates_done=1, gates_read=1, gate_steps=4,
                 gexp_done=1, gate_mix=6, gw_turned=1, gw_t_done=1, up1_done=2, h_stats=8, h_rstd=2, h_nm_done=1, z_act=2,
                 z_dve=2, z_turned=2, a_done=8, be_read=1, down1_done=2, k_stats=8, k_rstd=2, k_steps=2, u_done=4,
                 be_done=1, scaled=1, halved=1, base_done=1, summed=2, mix=1))
        s_fw = sem("s_fw")
        s_fset = sem("s_fset")
        s_fset2 = sem("s_fset2")

        def pick(t, b):
            if b.known:
                return t[b.off]
            v = t[bass.ds(b.times(1), 1)]
            return v.rearrange("a p n -> p (a n)") if len(t.shape) == 3 else v.rearrange("a p t n -> p (a t) n")

        def row(t, b):
            if b.known:
                return t[b.off]
            return t[bass.ds(b.times(1), 1)].rearrange("a p n -> p (a n)")

        block = es.enter_context(nc.Block())

        @block.sync
        def _(sp):
            sp.dma_start(cst[:], consts).then_inc(s_cst, 16)
            sp.dma_start(g_in[:], gates).then_inc(s_cst, 16)
            sp.dma_start(w_r[:], router).then_inc(s_cst, 16)
            slots_tiles = slots_d.rearrange("(t p) d -> p t d", p=P)
            zero_part = E0 * CAP // P // ZERO_PARTS

            def weights(e):
                if (e - 1).begun:
                    sp.wait_ge(z["wl_done"].of(e - 1), z["wl_done"].at(e - 1))
                if (e - 1).begun:
                    sp.wait_ge(z["wh_done"].of(e - 1), z["wh_done"].at(e - 1))
                half = w_raw[:, 0:C * F0], w_raw[:, C * F0:2 * C * F0]
                sp.dma_start(half[0], pick(w1_0, e).rearrange("p a n -> p (a n)")).then_inc(z["w_came"].sem, 16)
                sp.dma_start(half[1], pick(w2_0, e).rearrange("p a n -> p (a n)")).then_inc(z["w_came"].sem, 16)
                if At(e.pair, 3 * (e.off - 1) - 1, 6).begun:
                    sp.wait_ge(z["eo_done"].of(At(e.pair, 3 * (e.off - 1) - 1, 6)), z["eo_done"].at(At(e.pair, 3 * (e.off - 1) - 1, 6)))
                sp.dma_start(b1_in[:, e.parity, :], pick(b1_0, e)).then_inc(z["w_came"].sem, 16)
                sp.dma_start(b2_in[:, e.parity, :], pick(b2_0, e)).then_inc(z["w_came"].sem, 16)

            def layer1_weights():
                for dst, src in ((w1f, w1_1), (w2f, w2_1), (gw_in, gate_w), (gb_in, gate_b), (b12_in, b12_1), (g1_in, g1_1),
                                 (be1_in, be1_1), (g2_in, g2_1), (be2_in, be2_1)):
                    sp.dma_start(dst[:], src).then_inc(s_fw, 16)

            def attention_weights(n):
                for dst, src in ((w_q, wq), (w_k, wk), (w_v, wv), (w_p, wp)):
                    sp.dma_start(dst[:], src[n]).then_inc(s_w[n], 16)

            for n in range(2):
                y = sy[n]
                if n == 0:
                    attention_weights(0)
                if n == 0:
                    sp.dma_start(bp_g[:], b_proj).then_inc(s_bp, 16)
                x_src = x if n == 0 else x1_d
                res_src = x if n == 0 else x2_d
                dst_d = x1_d if n == 0 else x3_d

                def step(s):
                    if n == 0 and s.known and s.off < ZERO_PARTS // 2 - LEAD:
                        if s.off == -LEAD:
                            sp.wait_ge(s_zero_tile, 1)
                        for part in (2 * (s.off + LEAD), 2 * (s.off + LEAD) + 1):
                            sp.dma_start(slots_tiles[:, part * zero_part:(part + 1) * zero_part, :],
                                         zeros[:].unsqueeze(1).to_broadcast([P, zero_part, D])).then_inc(s_zeroed, 16)
                    if s.known and s.off == B - LEAD:
                        if n == 0:
                            weights(At(0, 0))
                        else:
                            layer1_weights()
                    b = s + 2
                    if b.within(B):
                        if n == 0:
                            if (b - 2).begun:
                                sp.wait_ge(y["xh_done"].of(b - 2), y["xh_done"].at(b - 2))
                        else:
                            if (b - 2).begun:
                                sp.wait_ge(y["x2_done"].of(b - 2), y["x2_done"].at(b - 2))
                        sp.dma_start(x_in[:, b.parity, :], row(x_src, b)).then_inc(y["x_came"].of(b), 16)
                        if n == 1:
                            if (b - 2).begun:
                                sp.wait_ge(y["y_came"].of(b - 2), y["y_came"].at(b - 2))
                            if (b - 2).begun:
                                sp.wait_ge(y["x2_done"].of(b - 2), y["x2_done"].at(b - 2))
                            sp.dma_start(slot_in[:, b.parity, :], row(slot_of_d, b)).then_inc(y["route_came"].of(b), 16)
                            sp.dma_start(weight_in[:, b.parity, :], row(weight_of_d, b)).then_inc(y["route_came"].of(b), 16)
                        if (b - 2).begun:
                            sp.wait_ge(y["in_turned"].of(b - 2), y["in_turned"].at(b - 2))
                        sp.dma_start(c_in[:, b.parity, :], row(ctx_in, b)).then_inc(y["c_came"].of(b), 16)
                    b = s + 1
                    if n == 1 and b.within(B):
                        sp.wait_ge(y["x2_done"].of(b), y["x2_done"].at(b))
                        sp.dma_start(row(x2_d, b), x2[:, b.parity, :]).then_inc(y["x2_stored"].of(b), 16)
                    b = s - 3
                    if b.within(B):
                        sp.wait_ge(y["x1_done"].of(b), y["x1_done"].at(b))
                        sp.dma_start(row(dst_d, b), x1[:, b.parity, :]).then_inc(y["x1_stored"].of(b), 16)
                    b = s - 1
                    if b.within(B):
                        if n == 1:
                            sp.wait_ge(y["x2_stored"].of(b), y["x2_stored"].at(b))
                        if (b - 2).begun:
                            sp.wait_ge(y["x1_done"].of(b - 2), y["x1_done"].at(b - 2))
                        sp.dma_start(x_res[:, b.parity, :], row(res_src, b)).then_inc(y["r_came"].of(b), 16)
                    b = s - 4
                    if n == 0 and b.within(B):
                        sp.wait_ge(y["slots_steps"].of(b), y["slots_steps"].at(b))
                        sp.dma_start(row(slot_of_d, b), slot_g[:, b.parity, :]).then_inc(y["route_stored"].of(b), 16)
                        sp.dma_start(row(weight_of_d, b), wgt[:, b.parity, :]).then_inc(y["route_stored"].of(b), 16)

                if n == 1:
                    for b in (B - 2, B - 1):
                        sp.wait_ge(sy[0]["x1_stored"].of(At(0, b)), sy[0]["x1_stored"].at(At(0, b)))
                        sp.wait_ge(sy[0]["route_stored"].of(At(0, b)), sy[0]["route_stored"].at(At(0, b)))
                run_steps(sp, B, LEAD, TAIL, WARM, step)
                for b in (B - 2, B - 1):
                    sp.wait_ge(y["x1_stored"].of(At(0, b)), y["x1_stored"].at(At(0, b)))
                    if n == 0:
                        sp.wait_ge(y["route_stored"].of(At(0, b)), y["route_stored"].at(At(0, b)))
                if n == 0:
                    for b in (B - 2, B - 1):
                        sp.wait_ge(sy[0]["scattered"].of(At(0, b)), sy[0]["scattered"].at(At(0, b)))
                    sp.wait_ge(sy[0]["slots_steps"].of(At(0, B - 1)), sy[0]["slots_steps"].at(At(0, B - 1)))

                    slots_v = slots_d.rearrange("(g t p) d -> g p t d", p=P, t=GT)
                    eo_v = eo_d.rearrange("(g t p) d -> g p t d", p=P, t=GT)

                    def slots(g):
                        if (g - 2).begun:
                            sp.wait_ge(z["g_turned"].of(g - 2), z["g_turned"].at(g - 2))
                        sp.dma_start(xg[:, g.parity], pick(slots_v, g)).then_inc(z["xg_came"].of(g), 16)

                    slots(At(0, 0))
                    sp.wait_ge(y["pr_done"].of(At(0, B - 1)), y["pr_done"].at(At(0, B - 1)))
                    attention_weights(1)

                    def estep(e, g, t):
                        if (g + 1).within(E0 * NG):
                            slots(g + 1)
                        if t == 0 and (e + 1).within(E0):
                            weights(e + 1)
                        sp.wait_ge(z["eo_done"].of(g), z["eo_done"].at(g))
                        sp.dma_start(pick(eo_v, g), eo[:, g.parity]).then_inc(z["eo_stored"].of(g), 16)

                    run_experts(sp, E0, estep)
                    for g in (E0 * NG - 2, E0 * NG - 1):
                        sp.wait_ge(z["eo_stored"].of(At(0, g)), z["eo_stored"].at(At(0, g)))

            def fstep(s):
                b = s - 3
                if b.within(B):
                    sp.wait_ge(f["mix"].of(b), f["mix"].at(b))
                    sp.dma_start(row(out, b), x4[:, b.parity, :]).then_inc(f["x4_stored"].of(b), 16)
                b = s + 2
                if b.within(B):
                    if (b - 2).begun:
                        sp.wait_ge(f["x3_came"].of(b - 2), f["x3_came"].at(b - 2))
                    if (b - 4).at_edge:
                        sp.wait_ge(f["base_done"].of(b - 4), f["base_done"].at(b - 4))
                    sp.dma_start(x3[:, b.off % 4, :], row(x3_d, b)).then_inc(f["x3_came"].of(b), 16)

            run_steps(sp, B, 2, 3, 8, fstep, 4)
            for b in (B - 2, B - 1):
                sp.wait_ge(f["x4_stored"].of(At(0, b)), f["x4_stored"].at(At(0, b)))

        @block.gpsimd
        def _(pool):
            def carrier():
                nc.gpsimd.tensor_tensor(pool_tick[:], neg_half[0:1], neg_half[0:1], ALU.mult)

            pool.memset(ones_bf[:], 1.0).then_inc(s_set, 1)
            pool.memset(base[:], 0.0).then_inc(s_set, 1)
            pool.memset(v_aug[:], 0.0).then_inc(s_vz, 1)
            pool.wait_ge(s_vz, 1)
            pool.memset(v_aug[:, :, :, DH:DH + 1], 1.0).then_inc(s_set, 1)
            for n in range(2):
                y = sy[n]

                def masked4(pool, dst, src, y):
                    nc.gpsimd.tensor_tensor(dst, src.unsqueeze(2).to_broadcast([P, 2, 2, P]),
                                            head_mask.unsqueeze(1).unsqueeze(3).to_broadcast([P, 2, 2, P]),
                                            ALU.mult).then_inc(y["masked"].sem, 1)

                def rstd(stats, mv, rs, steps, b):
                    pool.wait_ge(stats.of(b), stats.at(b))
                    if (b - 1).begun:
                        pool.wait_ge(steps.of(b - 1), steps.at(b - 1))
                    nc.gpsimd.tensor_tensor(rs[:, 0:1], mv[:, 1:2], eps, ALU.add).then_inc(steps.sem, 1)
                    pool.wait_ge(steps.of(b), steps.at(b, 1))
                    nc.gpsimd.tensor_tensor(rs[:, 1:2], rs[:, 0:1], neg_half, ALU.pow).then_inc(steps.sem, 1)

                def step(s):
                    b = s + 2
                    if n == 1 and b.within(B):
                        pool.wait_ge(y["route_came"].of(b), y["route_came"].at(b))
                        if (b - 2).begun:
                            pool.wait_ge(y["x2_done"].of(b - 2), y["x2_done"].at(b - 2))
                        if not b.known:
                            carrier()
                        pool.indirect_dma_start(
                            out=y_in[:, b.parity, :], out_offset=None, in_=eo_d,
                            in_offset=bass.IndirectOffsetOnAxis(ap=slot_in[:, b.parity, 0:1], axis=0),
                            bounds_check=E0 * CAP - 1, oob_is_err=False).then_inc(y["y_came"].of(b), 16)
                    b = s - 3
                    if n == 0 and b.within(B):
                        pool.wait_ge(y["x1_done"].of(b), y["x1_done"].at(b))
                        rstd(y["n2_stats"], mv2, rs2, y["n2_rstd"], b)
                    b = s + 1
                    if b.within(B):
                        if (b - 1).begun:
                            pool.wait_ge(y["xh_done"].of(b - 1), y["xh_done"].at(b - 1))
                        rstd(y["n1_stats"], mv1, rs1, y["n1_rstd"], b)
                    b = s - 2
                    if n == 0 and b.within(B):
                        pool.wait_ge(y["r_came"].of(b), y["r_came"].at(b))
                        if b.known and b.off == 0:
                            pool.wait_ge(s_bias, 1)
                        nc.gpsimd.tensor_tensor(x_res[:, b.parity, :], x_res[:, b.parity, :], bp_g[:], ALU.add)\
                            .then_inc(y["res_biased"].sem, 1)
                    b = s
                    if b.within(B):
                        p = b.parity
                        if (b - 2).begun:
                            pool.wait_ge(y["s2_done"].of(b - 2), y["s2_done"].at(b - 2))

                        pool.wait_ge(y["qk_hi_done"].of(b), y["qk_hi_done"].at(b))
                        masked4(pool, km_hi[:, p], qk_hi[:, p, 2:4, :], y)
                        masked4(pool, qm_hi[:, p], qk_hi[:, p, 0:2, :], y)
                        pool.wait_ge(y["qk_lo_done"].of(b), y["qk_lo_done"].at(b))
                        masked4(pool, qm_lo[:, p], qk_lo[:, p, 0:2, :], y)
                    b = s - 4
                    if n == 0 and b.within(B):
                        pool.wait_ge(y["slots_steps"].of(b), y["slots_steps"].at(b))
                        if not b.known:
                            carrier()
                        if b.known and b.off == 0:
                            pool.wait_ge(s_zeroed, 16 * ZERO_PARTS)
                        pool.indirect_dma_start(
                            out=slots_d, out_offset=bass.IndirectOffsetOnAxis(ap=slot_s[:, b.parity, 0:1], axis=0),
                            in_=xh2[:, b.parity, :], in_offset=None,
                            bounds_check=E0 * CAP - 1, oob_is_err=False).then_inc(y["scattered"].of(b), 16)

                run_steps(pool, B, LEAD, TAIL, WARM, step)
                if n == 0:
                    for b in (B - 2, B - 1):
                        pool.wait_ge(y["scattered"].of(At(0, b)), y["scattered"].at(At(0, b)))
                    for g in (E0 * NG - 2, E0 * NG - 1):
                        pool.wait_ge(z["eo_stored"].of(At(0, g)), z["eo_stored"].at(At(0, g)))

            def frstd(stats, mv, rs, steps, b, last_read):
                pool.wait_ge(stats.of(b), stats.at(b))
                if (b - 1).begun:
                    pool.wait_ge(last_read.of(b - 1), last_read.at(b - 1))
                nc.gpsimd.tensor_tensor(rs[:, 0, :], mv, eps.to_broadcast([P, rs.shape[2]]), ALU.add).then_inc(steps.sem, 1)
                pool.wait_ge(steps.of(b), steps.at(b, 1))
                nc.gpsimd.tensor_tensor(rs[:, 1, :], rs[:, 0, :], neg_half.to_broadcast([P, rs.shape[2]]), ALU.pow)\
                    .then_inc(steps.sem, 1)

            frs3 = frs[:].unsqueeze(2)

            def fstep(s):
                b = s - 3
                if b.within(B):
                    pool.wait_ge(f["u_done"].of(b), f["u_done"].at(b))
                    if (b - 1).begun:
                        pool.wait_ge(f["halved"].of(b - 1), f["halved"].at(b - 1))
                    nc.gpsimd.tensor_tensor(u2g[:], u2[:, b.parity], g2_in[:], ALU.mult).then_inc(f["scaled"].sem, 1)
                    pool.wait_ge(f["scaled"].of(b), f["scaled"].at(b))
                    if (b - 1).begun:
                        pool.wait_ge(f["mix"].of(b - 1), f["mix"].at(b - 1))
                    nc.gpsimd.tensor_tensor(u2s[:], u2g[:, 0:2, :], u2g[:, 2:4, :], ALU.add).then_inc(f["halved"].sem, 1)
                b = s - 2
                if b.within(B):
                    frstd(f["k_stats"], k_mv[:, :, 1], k_rs, f["k_rstd"], b, f["k_steps"])
                b = s - 3
                if b.within(B):
                    pool.wait_ge(f["be_read"].of(b), f["be_read"].at(b))
                    pool.wait_ge(f["base_done"].of(b), f["base_done"].at(b))
                    nc.gpsimd.tensor_tensor(mix2[:], mix1[:, b.off % 4, :], be_sb[:, b.parity, :], ALU.add).then_inc(f["summed"].sem, 1)
                    pool.wait_ge(f["halved"].of(b), f["halved"].at(b))
                    nc.gpsimd.tensor_tensor(u2t[:], u2s[:, 0, :], u2s[:, 1, :], ALU.add).then_inc(f["summed"].sem, 1)
                b = s
                if b.within(B):
                    frstd(f["h_stats"], h_mv[:, :, 1], h_rs, f["h_rstd"], b, f["z_dve"])
                b = s + 1
                if b.within(B):
                    frstd(f["st"], fmv[:, 1:2], frs3, f["rstd"], b, f["xf_done"])

            pool.wait_ge(s_fset2, 8)
            run_steps(pool, B, 2, 3, 8, fstep, 4)

        @block.scalar
        def _(act):
            act.wait_ge(s_cst, 48)
            nc.scalar.activation(g_t[:], g_in[:], ACT.Tanh).then_inc(s_tanh, 1)
            act.wait_ge(s_tanh, 1)
            act.wait_ge(s_bp, 16)
            nc.scalar.activation(bp_g[:], bp_g[:], ACT.Copy, scale=g_t[:, 0:1]).then_inc(s_bias, 1)
            for n in range(2):
                y = sy[n]
                act.wait_ge(s_w[n], 64)
                nc.scalar.activation(w_p[:], w_p[:], ACT.Copy, scale=g_t[:, n:n + 1]).then_inc(s_wp[n], 1)

                def exponentials(b, h):
                    act.wait_ge(y["s2_done"].of(b), y["s2_done"].at(b, h + 1))
                    nc.scalar.activation(prob_t[:, 8 * h:8 * h + 8, :].rearrange("p a k -> p (a k)"),
                                         scores[:, 2 * h:2 * h + 2, :].rearrange("p a k -> p (a k)"),
                                         ACT.Exp, scale=SOFT).then_inc(y["exp_done"].sem, 1)

                def step(s):
                    b = s
                    if b.within(B):
                        act.wait_ge(y["in_turned"].of(b), y["in_turned"].at(b))
                        if (b - 2).begun:
                            act.wait_ge(y["v_done"].of(b - 2), y["v_done"].at(b - 2))
                        nc.scalar.activation(in_t[:, b.parity].rearrange("p a k -> p (a k)"), b4, ACT.Copy).then_inc(y["in_t_done"].sem, 1)
                    b = s - 2
                    if b.within(B):
                        act.wait_ge(y["av_done"].of(b), y["av_done"].at(b))
                        if (b - 1).begun:
                            act.wait_ge(y["o1_done"].of(b - 1), y["o1_done"].at(b - 1))
                        nc.scalar.activation(o_pad[:].rearrange("p a k -> p (a k)"), b5, ACT.Copy).then_inc(y["o_pad_done"].sem, 1)
                    b = s
                    if b.within(B):
                        act.wait_ge(y["qk_done"].of(b), y["qk_done"].at(b))
                        if (b - 2).begun:
                            act.wait_ge(y["s2_done"].of(b - 2), y["s2_done"].at(b - 2))
                        if (b - 2).begun:
                            act.wait_ge(y["masked"].of(b - 2), y["masked"].at(b - 2))
                        nc.scalar.activation(qk_hi[:, b.parity].rearrange("p a k -> p (a k)"), b5, ACT.Copy).then_inc(y["qk_hi_done"].sem, 1)
                        act.wait_ge(y["v_done"].of(b), y["v_done"].at(b))
                        if (b - 2).begun:
                            act.wait_ge(y["av_done"].of(b - 2), y["av_done"].at(b - 2))
                        nc.scalar.activation(v_aug[:, b.parity, :, 0:DH], b6[:, 0:D].rearrange("p (h d) -> p h d", h=H),
                                             ACT.Copy).then_inc(y["v_out"].sem, 1)
                    b = s - 4
                    if n == 0 and b.within(B):
                        act.wait_ge(y["top_done"].of(b), y["top_done"].at(b))
                        if (b - 1).begun:
                            act.wait_ge(y["den_done"].of(b - 1), y["den_done"].at(b - 1))
                        nc.scalar.activation(ex8[:], lg[:, b.parity, :], ACT.Exp, bias=ntop[:, b.parity, 0:1],
                                             accum_out=den8[:, b.parity, 0:1]).then_inc(y["den_done"].sem, 1)
                    b = s - 3
                    if n == 0 and b.within(B):
                        act.wait_ge(y["x2_turned"].of(b), y["x2_turned"].at(b))
                        if (b - 2).begun:
                            act.wait_ge(y["lg_done"].of(b - 2), y["lg_done"].at(b - 2))
                        nc.scalar.activation(x2_t[:, b.parity].rearrange("p a k -> p (a k)"), b6[:, 0:D], ACT.Copy).then_inc(y["x2_t_done"].sem, 1)
                    b = s - 1
                    if b.within(B):
                        if (b - 1).begun:
                            act.wait_ge(y["av_done"].of(b - 1), y["av_done"].at(b - 1))
                        exponentials(b, 0)
                    b = s - 2
                    if b.within(B):
                        act.wait_ge(y["o2_done"].of(b), y["o2_done"].at(b))
                        if (b - 2).begun:
                            act.wait_ge(y["pr_done"].of(b - 2), y["pr_done"].at(b - 2))
                        nc.scalar.activation(o_t[:, b.parity].rearrange("p a k -> p (a k)"), b7[:, 0:D], ACT.Copy).then_inc(y["o_t_done"].sem, 1)
                    b = s - 1
                    if b.within(B):
                        exponentials(b, 1)

                run_steps(act, B, LEAD, TAIL, WARM, step)
                if n == 0:
                    def split_weights(e):
                        act.wait_ge(z["w_came"].of(e), z["w_came"].at(e))
                        if At(e.pair, 3 * (e.off - 1) - 1, 6).begun:
                            act.wait_ge(z["down_done"].of(At(e.pair, 3 * (e.off - 1) - 1, 6)), z["down_done"].at(At(e.pair, 3 * (e.off - 1) - 1, 6)))
                        nc.scalar.activation(w_hi[:, e.parity], w_raw[:], ACT.Copy).then_inc(z["wh_done"].sem, 1)

                    def turned(g):
                        for c in range(C):
                            act.wait_ge(z["g_turned"].of(g), z["g_turned"].at(g, c + 1))
                            if c == 0:
                                if (g - 2).begun:
                                    act.wait_ge(z["up_done"].of(g - 2), z["up_done"].at(g - 2))
                            nc.scalar.activation(xgt_hi[:, g.parity, c, :], ps[:, 6 + c, 0:G], ACT.Copy)\
                                .then_inc(z["xg_hi_done"].sem, 1)

                    split_weights(At(0, 0))
                    act.wait_ge(sy[0]["slots_steps"].of(At(0, B - 1)), sy[0]["slots_steps"].at(At(0, B - 1)))
                    turned(At(0, 0))

                    def estep(e, g, t):
                        for fc in range(FC):
                            act.wait_ge(z["up_done"].of(g), z["up_done"].at(g, fc + 1))
                            if fc >= 2:
                                act.wait_ge(z["hid_lo_done"].of(g), z["hid_lo_done"].at(g, fc - 1))
                            else:
                                if (g - 1).begun:
                                    act.wait_ge(z["hid_lo_done"].of(g - 1), z["hid_lo_done"].at(g - 1, FC - 1 + fc))
                            nc.scalar.activation(hid[:, fc % 2, :], ps[:, 4 + fc % 2, 0:G], ACT.Gelu,
                                                 bias=b1_in[:, e.parity, fc:fc + 1]).then_inc(z["hid_done"].sem, 1)
                        if (g + 1).within(E0 * NG):
                            turned(g + 1)
                        if t == 1 and (e + 1).within(E0):
                            split_weights(e + 1)

                    run_experts(act, E0, estep)

            act.wait_ge(s_fw, 16 * 9)
            nc.scalar.activation(w1_hi[:], w1f[:], ACT.Copy).then_inc(s_fset, 1)
            nc.scalar.activation(gw_hi[:], gw_in[:], ACT.Copy).then_inc(s_fset, 1)
            nc.scalar.activation(b12_hi[:], b12_in[:], ACT.Copy).then_inc(s_fset, 1)
            nc.scalar.activation(be2_in[:], be2_in[:], ACT.Copy, scale=g_t[0:E1, 3:4]).then_inc(s_fset, 1)
            act.wait_ge(s_fset, 4)

            def fstep(s):
                b = s
                if b.within(B):
                    act.wait_ge(f["x_turned"].of(b), f["x_turned"].at(b))
                    if (b - 2).begun:
                        act.wait_ge(f["gates_done"].of(b - 2), f["gates_done"].at(b - 2))
                    nc.scalar.activation(xft_hi[:, b.parity].rearrange("p c k -> p (c k)"), ps[:, 0, 0:D], ACT.Copy)\
                        .then_inc(f["x_hi_done"].sem, 1)
                b = s - 1
                if b.within(B):
                    if (b - 2).begun:
                        act.wait_ge(f["down1_done"].of(b - 2), f["down1_done"].at(b - 2))
                    for e in range(E1):
                        if e % 2 == 0:
                            act.wait_ge(f["z_turned"].of(b), f["z_turned"].at(b, e // 2 + 1))
                        for c in range(C):
                            nc.scalar.activation(a_t[:, b.parity, e, c, :], ps[:, 4 + e // 2, (e % 2 * 2 + c) * P:(e % 2 * 2 + c + 1) * P],
                                                 ACT.Relu, scale=g1_in[:, e, c:c + 1], bias=be1_in[:, e, c:c + 1])\
                                .then_inc(f["a_done"].sem, 1)
                b = s - 2
                if b.within(B):
                    act.wait_ge(f["be_done"].of(b), f["be_done"].at(b))
                    if (b - 2).begun:
                        act.wait_ge(f["mix"].of(b - 2), f["mix"].at(b - 2))
                    nc.scalar.activation(be_sb[:, b.parity, :], ps[:, 1, 256:512], ACT.Copy).then_inc(f["be_read"].sem, 1)
                    act.wait_ge(f["k_steps"].of(b), f["k_steps"].at(b))
                    if (b - 2).begun:
                        act.wait_ge(f["scaled"].of(b - 2), f["scaled"].at(b - 2))
                    for e in range(E1):
                        nc.scalar.activation(u2[:, b.parity, e, :], ps[:, 6 + e // 2, (e % 2) * D:(e % 2 + 1) * D], ACT.Identity,
                                             scale=k_rw[:, e:e + 1], bias=k_nm[:, e:e + 1]).then_inc(f["u_done"].sem, 1)
                b = s - 1
                if b.within(B):
                    act.wait_ge(f["gw_turned"].of(b), f["gw_turned"].at(b))
                    if (b - 2).begun:
                        act.wait_ge(f["be_done"].of(b - 2), f["be_done"].at(b - 2))
                    nc.scalar.activation(gwt_t[:, b.parity, :], ps[0:E1, 1, 0:P], ACT.Copy).then_inc(f["gw_t_done"].sem, 1)
                b = s
                if b.within(B):
                    act.wait_ge(f["h_nm_done"].of(b), f["h_nm_done"].at(b))
                    if (b - 2).begun:
                        act.wait_ge(f["z_turned"].of(b - 2), f["z_turned"].at(b - 2))
                    for e in range(2):
                        nc.scalar.activation(z1[:, b.parity, e, :], ps[:, 2, e * D:(e + 1) * D], ACT.Identity,
                                             scale=h_rs[:, 1, e:e + 1], bias=h_nm[:, e:e + 1]).then_inc(f["z_act"].sem, 1)
                    act.wait_ge(f["gate_steps"].of(b), f["gate_steps"].at(b))
                    if (b - 1).begun:
                        act.wait_ge(f["gate_mix"].of(b - 1), f["gate_mix"].at(b - 1))
                    nc.scalar.activation(gexp[:], gdiff[:], ACT.Exp).then_inc(f["gexp_done"].sem, 1)

            run_steps(act, B, 2, 3, 8, fstep, 4)

        @block.tensor
        def _(pe):
            pe.wait_ge(s_cst, 48)
            pe.wait_ge(s_cst2, 3)
            pe.wait_ge(s_set, 3)

            for n in range(2):
                y = sy[n]
                pe.wait_ge(s_w[n], 64)
                pe.wait_ge(s_wp[n], 1)

                def scores_half(b, half):
                    p = b.parity
                    for j in (2 * half, 2 * half + 1):
                        pe.matmul(scores[:, j, :], quad_ones[:, j, :], nmax_x[:, p].rearrange("p a k -> p (a k)"),
                                  start=True, stop=False, skip_group_check=True)
                    for hf in range(2):
                        for k_part, q_part in ((qk_hi, qm_hi), (qk_lo, qm_hi), (qk_hi, qm_lo)):
                            for j in (2 * half, 2 * half + 1):
                                r0 = 32 * j
                                mm = pe.matmul(scores[:, j, hf * 256:(hf + 1) * 256], k_part[r0:r0 + 32, p, 2 + hf, :],
                                               q_part[r0:r0 + 32, p, hf, :, :].rearrange("p m k -> p (m k)"),
                                               start=False, stop=True, skip_group_check=True)
                    mm.then_inc(y["s2_done"].sem, 1)

                def step(s):
                    b = s
                    if b.within(B):
                        p = b.parity
                        pe.wait_ge(y["c_came"].of(b), y["c_came"].at(b))
                        pe.wait_ge(y["xh_done"].of(b), y["xh_done"].at(b))
                        if (b - 3).begun:
                            pe.wait_ge(y["o_norm"].of(b - 3), y["o_norm"].at(b - 3))
                        if (b - 1).at_edge:
                            pe.wait_ge(y["in_t_done"].of(b - 1), y["in_t_done"].at(b - 1))
                        for c in range(C):
                            pe.transpose(b4[:, c * P:(c + 1) * P], c_in[:, p, c * P:(c + 1) * P], ident)
                        for c in range(C):
                            mm = pe.transpose(b4[:, (2 + c) * P:(3 + c) * P], xh[:, p, c * P:(c + 1) * P], ident)
                        mm.then_inc(y["in_turned"].sem, 1)
                    b = s - 2
                    if b.within(B):
                        p = b.parity
                        if (b + 1).within(B):
                            pe.wait_ge(y["qk_lo_done"].of(b + 1), y["qk_lo_done"].at(b + 1))
                        else:
                            if (b - 1).at_edge:
                                pe.wait_ge(y["o_pad_done"].of(b - 1), y["o_pad_done"].at(b - 1))
                        pe.wait_ge(y["v_out"].of(b), y["v_out"].at(b))
                        for r in range(H):
                            if r % 8 == 0:
                                pe.wait_ge(y["exp_done"].of(b), y["exp_done"].at(b, r // 8 + 1))
                            j, g = r // 4, r % 4
                            h = 8 * (g // 2) + 2 * j + g % 2
                            mm = pe.matmul(b5[32 * g:32 * g + 32, j * P:(j + 1) * P], v_aug[:, p, h, :], prob_t[:, r, :],
                                           start=True, stop=True, tile_position=(0, 32 * g))
                        mm.then_inc(y["av_done"].sem, 1)
                    b = s - 1
                    if b.within(B):
                        p = b.parity
                        pe.wait_ge(y["masked"].of(b), y["masked"].at(b))
                        if (b - 1).begun:
                            pe.wait_ge(y["exp_done"].of(b - 1), y["exp_done"].at(b - 1))
                        for hf in range(2):
                            for j in range(HP):
                                r0 = 32 * j
                                mm = pe.matmul(scores[:, j, hf * 256:(hf + 1) * 256], qk_hi[r0:r0 + 32, p, hf, :],
                                               km_hi[r0:r0 + 32, p, hf, :, :].rearrange("p m k -> p (m k)"),
                                               start=True, stop=True)
                        mm.then_inc(y["s1_done"].sem, 1)
                    b = s
                    if b.within(B):
                        p = b.parity
                        pe.wait_ge(y["in_t_done"].of(b), y["in_t_done"].at(b))
                        if (b - 2).begun:
                            pe.wait_ge(y["o_pad_done"].of(b - 2), y["o_pad_done"].at(b - 2))
                        if (b - 1).at_edge:
                            pe.wait_ge(y["qk_lo_done"].of(b - 1), y["qk_lo_done"].at(b - 1))
                        for w, part, src in ((w_q, 0, 2), (w_k, 2, 0)):
                            for m in range(C):
                                for c in range(C):
                                    mm = pe.matmul(b5[:, (part + m) * P:(part + m + 1) * P], w[:, c, m * P:(m + 1) * P],
                                                   in_t[:, p, src + c, :], start=(c == 0), stop=(c == C - 1))
                        mm.then_inc(y["qk_done"].sem, 1)
                        if (b - 3).begun:
                            pe.wait_ge(y["x1_done"].of(b - 3), y["x1_done"].at(b - 3))
                        if (b - 1).at_edge:
                            pe.wait_ge(y["v_out"].of(b - 1), y["v_out"].at(b - 1))
                        for c in range(C):
                            mm = pe.matmul(b6[:, 0:D], in_t[:, p, c, :], w_v[:, c, :], start=(c == 0), stop=(c == C - 1))
                        mm.then_inc(y["v_done"].sem, 1)
                    b = s - 1
                    if b.within(B):
                        pe.wait_ge(y["max_done"].of(b), y["max_done"].at(b))
                        if n == 0 and (b - 3).begun:
                            pe.wait_ge(y["lg_read"].of(b - 3), y["lg_read"].at(b - 3))
                        elif (b - 2).begun:
                            pe.wait_ge(y["o_t_done"].of(b - 2), y["o_t_done"].at(b - 2))
                        elif (b - 1).begun:
                            pe.wait_ge(y["nmax_done"].of(b - 1), y["nmax_done"].at(b - 1))
                        pe.transpose(b7[0:H, 0:P], nmax[:, b.parity, :], ident).then_inc(y["max_turned"].sem, 1)
                    b = s - 2
                    if b.within(B):
                        pe.wait_ge(y["o_pad_done"].of(b), y["o_pad_done"].at(b))
                        if (b + 2).within(B):
                            pe.wait_ge(y["in_t_done"].of(b + 2), y["in_t_done"].at(b + 2))
                        else:
                            if (b - 1).at_edge:
                                pe.wait_ge(y["o_norm"].of(b - 1), y["o_norm"].at(b - 1))
                        for j in range(4):
                            mm = pe.transpose(b4[:, j * P:(j + 1) * P], o_pad[:, j, :], ident)
                        mm.then_inc(y["o1_done"].sem, 1)
                    b = s - 3
                    if n == 0 and b.within(B):
                        pe.wait_ge(y["xh2_done"].of(b), y["xh2_done"].at(b))
                        if (b + 3).within(B):
                            pe.wait_ge(y["v_out"].of(b + 3), y["v_out"].at(b + 3))
                        for c in range(C):
                            mm = pe.transpose(b6[:, c * P:(c + 1) * P], xh2[:, b.parity, c * P:(c + 1) * P], ident)
                        mm.then_inc(y["x2_turned"].sem, 1)
                    b = s - 4
                    if n == 0 and b.within(B):
                        pe.wait_ge(y["top_done"].of(b), y["top_done"].at(b))
                        if (b + 3).within(B):
                            pe.wait_ge(y["nmax_done"].of(b + 3), y["nmax_done"].at(b + 3))
                        pe.matmul(b7[:, 272:272 + E0], tri[:], onehot[:, b.parity, :], start=True, stop=True)
                        pe.matmul(b7[:, 288:288 + E0], ones_bf[:], onehot[:, b.parity, :], start=True, stop=True)\
                            .then_inc(y["cum_done"].sem, 1)
                    b = s - 1
                    if b.within(B):
                        pe.wait_ge(y["nmax_done"].of(b), y["nmax_done"].at(b))
                        scores_half(b, 0)
                    b = s - 2
                    if b.within(B):
                        pe.wait_ge(y["o_norm"].of(b), y["o_norm"].at(b))
                        if n == 0 and (b - 2).begun:
                            pe.wait_ge(y["cum_read"].of(b - 2), y["cum_read"].at(b - 2))
                        elif (b + 1).within(B):
                            pe.wait_ge(y["nmax_done"].of(b + 1), y["nmax_done"].at(b + 1))
                        elif (b - 1).begun:
                            pe.wait_ge(y["o_t_done"].of(b - 1), y["o_t_done"].at(b - 1))
                        for c in range(C):
                            mm = pe.transpose(b7[:, c * P:(c + 1) * P],
                                              o_n[:, b.parity].rearrange("p h d -> p (h d)")[:, c * P:(c + 1) * P], ident)
                        mm.then_inc(y["o2_done"].sem, 1)
                    b = s - 1
                    if b.within(B):
                        scores_half(b, 1)
                    b = s - 3
                    if n == 0 and b.within(B):
                        pe.wait_ge(y["x2_t_done"].of(b), y["x2_t_done"].at(b))
                        if (b + 1).within(B):
                            pe.wait_ge(y["o_t_done"].of(b + 1), y["o_t_done"].at(b + 1))
                        elif (b - 1).begun:
                            pe.wait_ge(y["cum_read"].of(b - 1), y["cum_read"].at(b - 1))
                        for c in range(C):
                            mm = pe.matmul(b7[:, 256:256 + E0], x2_t[:, b.parity, c, :], w_r[:, c, :],
                                           start=(c == 0), stop=(c == C - 1))
                        mm.then_inc(y["lg_done"].sem, 1)
                    b = s - 2
                    if b.within(B):
                        pe.wait_ge(y["o_t_done"].of(b), y["o_t_done"].at(b))
                        if n == 0:
                            if (b - 1).begun:
                                pe.wait_ge(y["x2_t_done"].of(b - 1), y["x2_t_done"].at(b - 1))
                        if (b + 2).within(B):
                            pe.wait_ge(y["v_out"].of(b + 2), y["v_out"].at(b + 2))
                        for c in range(C):
                            mm = pe.matmul(b6[:, 0:D], o_t[:, b.parity, c, :], w_p[:, c, :], start=(c == 0), stop=(c == C - 1))
                        mm.then_inc(y["pr_done"].sem, 1)

                run_steps(pe, B, LEAD, TAIL, WARM, step)
                if n == 0:
                    pe.wait_ge(sy[0]["slots_steps"].of(At(0, B - 1)), sy[0]["slots_steps"].at(At(0, B - 1)))

                    def turn(g):
                        pe.wait_ge(z["xg_came"].of(g), z["xg_came"].at(g))
                        if (g - 1).begun:
                            pe.wait_ge(z["xg_lo_done"].of(g - 1), z["xg_lo_done"].at(g - 1))
                        for c in range(C):
                            for t in range(GT):
                                mm = pe.transpose(ps[:, 6 + c, t * P:(t + 1) * P], xg[:, g.parity, t, c * P:(c + 1) * P], ident)
                            mm.then_inc(z["g_turned"].sem, 1)

                    turn(At(0, 0))

                    def estep(e, g, t):
                        q = e.parity
                        if t == 0:
                            pe.wait_ge(z["wh_done"].of(e), z["wh_done"].at(e))
                            pe.wait_ge(z["wl_done"].of(e), z["wl_done"].at(e))
                        pe.wait_ge(z["xg_lo_done"].of(g), z["xg_lo_done"].at(g))
                        for fc in range(FC):
                            if fc >= 2:
                                pe.wait_ge(z["hid_done"].of(g), z["hid_done"].at(g, fc - 1))
                            else:
                                if (g - 1).begun:
                                    pe.wait_ge(z["hid_done"].of(g - 1), z["hid_done"].at(g - 1, FC - 1 + fc))
                            k = 0
                            for c in range(C):
                                at = c * F0 + fc * P
                                for w, xt in ((w_hi, xgt_hi), (w_hi, xgt_lo), (w_lo, xgt_hi)):
                                    mm = pe.matmul(ps[:, 4 + fc % 2, 0:G], w[:, q, at:at + P], xt[:, g.parity, c, :],
                                                   start=(k == 0), stop=(k == 5))
                                    k += 1
                            mm.then_inc(z["up_done"].sem, 1)
                        if (g + 1).within(E0 * NG):
                            turn(g + 1)
                        for fc in range(FC):
                            pe.wait_ge(z["hid_lo_done"].of(g), z["hid_lo_done"].at(g, fc + 1))
                            at = C * F0 + fc * D
                            for i in range(GT):
                                if fc == 0:
                                    if (g - 1).begun:
                                        pe.wait_ge(z["eo_done"].of(g - 1), z["eo_done"].at(g - 1, i + 1))
                                for k, (hd, w) in enumerate(((hid_hi, w_hi), (hid_hi, w_lo), (hid_lo, w_hi))):
                                    mm = pe.matmul(ps[:, i, 0:D], hd[:, fc, i * P:(i + 1) * P], w[:, q, at:at + D],
                                                   start=(fc == 0 and k == 0), stop=(fc == FC - 1 and k == 2))
                        mm.then_inc(z["down_done"].sem, 1)

                    run_experts(pe, E0, estep)

            pe.wait_ge(y1["x1_done"].of(At(0, B - 1)), y1["x1_done"].at(At(0, B - 1)))
            pe.wait_ge(s_fset, 4)
            pe.wait_ge(s_fset2, 8)

            def bias_row(dst, which, e):
                pe.matmul(dst, ones2[:], b12[:, which, e, :], start=True, stop=False, skip_group_check=True)

            def fstep(s):
                b = s
                if b.within(B):
                    pe.wait_ge(f["xf_done"].of(b), f["xf_done"].at(b))
                    if (b - 1).begun:
                        pe.wait_ge(f["gates_read"].of(b - 1), f["gates_read"].at(b - 1))
                    for c in range(C):
                        mm = pe.transpose(ps[:, 0, c * P:(c + 1) * P], xf[:, b.off % 4, c * P:(c + 1) * P], ident)
                    mm.then_inc(f["x_turned"].sem, 1)
                b = s - 1
                if b.within(B):
                    pe.wait_ge(f["z_act"].of(b), f["z_act"].at(b))
                    pe.wait_ge(f["z_dve"].of(b), f["z_dve"].at(b))
                    if (b - 1).begun:
                        pe.wait_ge(f["a_done"].of(b - 1), f["a_done"].at(b - 1))
                    for e in range(E1):
                        for c in range(C):
                            mm = pe.transpose(ps[:, 4 + e // 2, (e % 2 * 2 + c) * P:(e % 2 * 2 + c + 1) * P],
                                              z1[:, b.parity, e, c * P:(c + 1) * P], ident)
                        if e % 2 == 1:
                            mm.then_inc(f["z_turned"].sem, 1)
                b = s - 2
                if b.within(B):
                    pe.wait_ge(f["gw_t_done"].of(b), f["gw_t_done"].at(b))
                    pe.matmul(ps[:, 1, 256:512], gwt_t[:, b.parity, :], be2_in[:], start=True, stop=True).then_inc(f["be_done"].sem, 1)
                b = s
                if b.within(B):
                    pe.wait_ge(f["x_lo_done"].of(b), f["x_lo_done"].at(b))
                    if (b - 1).begun:
                        pe.wait_ge(f["z_act"].of(b - 1), f["z_act"].at(b - 1))
                    if (b - 1).begun:
                        pe.wait_ge(f["z_dve"].of(b - 1), f["z_dve"].at(b - 1))
                    for e in range(E1):
                        dst = ps[:, 2 + e // 2, (e % 2) * D:(e % 2 + 1) * D]
                        bias_row(dst, 0, e)
                        for c in range(C):
                            for xt, w in ((xft_hi, w1_hi), (xft_hi, w1_lo), (xft_lo, w1_hi)):
                                mm = pe.matmul(dst, xt[:, b.parity, c, :], w[:, e, c, :], start=False, stop=True, skip_group_check=True)
                        if e % 2 == 1:
                            mm.then_inc(f["up1_done"].sem, 1)
                    k = 0
                    for c in range(C):
                        for xt, w in ((xft_hi, gw_hi), (xft_hi, gw_lo), (xft_lo, gw_hi)):
                            mm = pe.matmul(ps[:, 0, 256:256 + E1], xt[:, b.parity, c, :], w[:, c, :], start=(k == 0), stop=(k == 5))
                            k += 1
                    mm.then_inc(f["gates_done"].sem, 1)
                b = s - 1
                if b.within(B):
                    pe.wait_ge(f["gate_mix"].of(b), f["gate_mix"].at(b))
                    if (b - 1).begun:
                        pe.wait_ge(f["be_read"].of(b - 1), f["be_read"].at(b - 1))
                    pe.transpose(ps[0:E1, 1, 0:P], gwt[:, b.parity, :], ident).then_inc(f["gw_turned"].sem, 1)
                    if (b - 1).begun:
                        pe.wait_ge(f["u_done"].of(b - 1), f["u_done"].at(b - 1))
                    for e in range(E1):
                        if e % 2 == 0:
                            pe.wait_ge(f["a_done"].of(b), f["a_done"].at(b, 4 * (e // 2) + 4))
                        dst = ps[:, 6 + e // 2, (e % 2) * D:(e % 2 + 1) * D]
                        bias_row(dst, 1, e)
                        for c in range(C):
                            mm = pe.matmul(dst, a_t[:, b.parity, e, c, :], w2f[:, e, c, :], start=False, stop=True, skip_group_check=True)
                        if e % 2 == 1:
                            mm.then_inc(f["down1_done"].sem, 1)

            run_steps(pe, B, 2, 3, 8, fstep, 4)

        @block.vector
        def _(dve):
            def carrier():
                dve.memset(dve_tick[:], 0.0)

            dve.memset(zeros[:], 0.0).then_inc(s_zero_tile, 1)
            dve.memset(nmax_x[:].bitcast(F32), 0.0).then_inc(s_cst2, 1)
            dve.wait_ge(s_cst, 48)
            nc.vector.tensor_copy(tri[:], tri_f).then_inc(s_cst2, 1)
            nc.vector.tensor_copy(quad_ones[:], quad_rows.unsqueeze(2).to_broadcast([P, 4, P])).then_inc(s_cst2, 1)
            dve.wait_ge(s_cst2, 3)
            dve.wait_ge(s_set, 3)
            dve.wait_ge(s_tanh, 1)
            for n in range(2):
                y = sy[n]

                def step(s):
                    b = s - 3
                    if b.within(B):
                        p = b.parity
                        dve.wait_ge(y["pr_done"].of(b), y["pr_done"].at(b))
                        if n == 0:
                            dve.wait_ge(y["res_biased"].of(b), y["res_biased"].at(b))
                        else:
                            dve.wait_ge(y["r_came"].of(b), y["r_came"].at(b))
                        if (b - 2).begun:
                            dve.wait_ge(y["x1_stored"].of(b - 2), y["x1_stored"].at(b - 2))
                        nc.vector.tensor_tensor(x1[:, p, :], b6[:, 0:D], x_res[:, p, :], ALU.add).then_inc(y["x1_done"].sem, 1)
                        if n == 0:
                            dve.wait_ge(y["x1_done"].of(b), y["x1_done"].at(b))
                            nc.vector.bn_stats(st2[:], x1[:, p, :]).then_inc(y["n2_stats"].sem, 1)
                            dve.wait_ge(y["n2_stats"].of(b), y["n2_stats"].at(b, 1))
                            if not b.known:
                                carrier()
                            nc.vector.bn_aggr(mv2[:], st2[:]).then_inc(y["n2_stats"].sem, 1)
                    b = s + 1
                    if b.within(B):
                        p = b.parity
                        dve.wait_ge(y["x_came"].of(b), y["x_came"].at(b))
                        src = x_in
                        if n == 1:
                            src = x2
                            dve.wait_ge(y["y_came"].of(b), y["y_came"].at(b))
                            dve.wait_ge(y["route_came"].of(b), y["route_came"].at(b))
                            if (b - 2).begun:
                                dve.wait_ge(y["x2_stored"].of(b - 2), y["x2_stored"].at(b - 2))
                            nc.vector.scalar_tensor_tensor(out=x2[:, p, :], in0=y_in[:, p, :], scalar=weight_in[:, p, 0:1],
                                                           in1=x_in[:, p, :], op0=ALU.mult, op1=ALU.add).then_inc(y["x2_done"].sem, 1)
                            dve.wait_ge(y["x2_done"].of(b), y["x2_done"].at(b))
                        nc.vector.bn_stats(st1[:], src[:, p, :]).then_inc(y["n1_stats"].sem, 1)
                        dve.wait_ge(y["n1_stats"].of(b), y["n1_stats"].at(b, 1))
                        if not b.known:
                            carrier()
                        nc.vector.bn_aggr(mv1[:], st1[:]).then_inc(y["n1_stats"].sem, 1)
                    b = s - 1
                    if b.within(B):
                        dve.wait_ge(y["s1_done"].of(b), y["s1_done"].at(b))
                        if (b - 2).begun:
                            dve.wait_ge(y["max_turned"].of(b - 2), y["max_turned"].at(b - 2))
                        for h in range(2):
                            nc.vector.tensor_reduce(nmax[:, b.parity, 8 * h:8 * h + 8],
                                                    scores[:, 2 * h:2 * h + 2, :].rearrange("p a (r k) -> p (a r) k", k=P),
                                                    AX_X, ALU.max, negate=True).then_inc(y["max_done"].sem, 1)
                    b = s - 3
                    if n == 0 and b.within(B):
                        p = b.parity
                        dve.wait_ge(y["n2_rstd"].of(b), y["n2_rstd"].at(b))
                        if (b - 2).begun:
                            dve.wait_ge(y["scattered"].of(b - 2), y["scattered"].at(b - 2))
                        nc.vector.tensor_scalar(xh2[:, p, :], x1[:, p, :], mv2[:, 0:1], rs2[:, 1:2], ALU.subtract, ALU.mult)\
                            .then_inc(y["xh2_done"].sem, 1)
                    b = s - 1
                    if b.within(B):
                        dve.wait_ge(y["max_turned"].of(b), y["max_turned"].at(b))
                        if (b - 2).begun:
                            dve.wait_ge(y["s2_done"].of(b - 2), y["s2_done"].at(b - 2))
                        nc.vector.tensor_tensor(nmax_x[0:H, b.parity], b7[0:H, 0:P].unsqueeze(1).to_broadcast([H, 4, P]),
                                                row_mask.unsqueeze(2).to_broadcast([H, 4, P]), ALU.mult).then_inc(y["nmax_done"].sem, 1)
                    b = s + 1
                    if b.within(B):
                        p = b.parity
                        dve.wait_ge(y["n1_rstd"].of(b), y["n1_rstd"].at(b))
                        if (b - 2).begun:
                            dve.wait_ge(y["in_turned"].of(b - 2), y["in_turned"].at(b - 2))
                        src = x_in if n == 0 else x2
                        nc.vector.tensor_scalar(xh[:, p, :], src[:, p, :], mv1[:, 0:1], rs1[:, 1:2], ALU.subtract, ALU.mult)\
                            .then_inc(y["xh_done"].sem, 1)
                    b = s
                    if b.within(B):
                        p = b.parity
                        dve.wait_ge(y["qk_hi_done"].of(b), y["qk_hi_done"].at(b))
                        if (b - 2).begun:
                            dve.wait_ge(y["s2_done"].of(b - 2), y["s2_done"].at(b - 2))
                        if (b - 2).begun:
                            dve.wait_ge(y["masked"].of(b - 2), y["masked"].at(b - 2))
                        nc.vector.tensor_tensor(qk_lo[:, p].rearrange("p a k -> p (a k)"), b5,
                                                qk_hi[:, p].rearrange("p a k -> p (a k)"), ALU.subtract).then_inc(y["qk_lo_done"].sem, 1)
                    b = s - 2
                    if b.within(B):
                        p = b.parity
                        dve.wait_ge(y["o1_done"].of(b), y["o1_done"].at(b))
                        if (b - 2).begun:
                            dve.wait_ge(y["o2_done"].of(b - 2), y["o2_done"].at(b - 2))
                        o_q = b4.rearrange("p (r c) -> p r c", c=32)
                        nc.vector.reciprocal(rden[:].unsqueeze(2), o_q[:, :, DH:DH + 1]).then_inc(y["o_norm"].sem, 1)
                        dve.wait_ge(y["o_norm"].of(b), y["o_norm"].at(b, 1))
                        nc.vector.tensor_tensor(o_n[:, p], o_q[:, :, 0:DH], rden[:].unsqueeze(2).to_broadcast([P, H, DH]), ALU.mult)\
                            .then_inc(y["o_norm"].sem, 1)
                    b = s - 4
                    if n == 0 and b.within(B):
                        p = b.parity
                        st = y["slots_steps"]

                        dve.wait_ge(y["cum_done"].of(b), y["cum_done"].at(b))
                        nc.vector.tensor_tensor(cum[:], b7[:, 272:272 + E0], base[:], ALU.add).then_inc(st.sem, 1)
                        dve.wait_ge(st.of(b), st.at(b, 1))
                        nc.vector.tensor_tensor(base[:], b7[:, 288:288 + E0], base[:], ALU.add).then_inc(y["cum_read"].sem, 1)
                        dve.wait_ge(y["cum_read"].of(b), y["cum_read"].at(b))
                        nc.vector.tensor_tensor_reduce(cumsel[:], cum[:], onehot[:, p, :], 1.0, 0.0, ALU.mult, ALU.add, pos[:]).then_inc(st.sem, 1)
                        dve.wait_ge(st.of(b), st.at(b, 2))
                        nc.vector.tensor_scalar(kept[:], pos[:], float(CAP), None, ALU.is_le).then_inc(st.sem, 1)
                        dve.wait_ge(st.of(b), st.at(b, 3))
                        nc.vector.tensor_scalar(posc[:], pos[:], float(CAP), -1.0, ALU.min, ALU.add).then_inc(st.sem, 1)
                        dve.wait_ge(st.of(b), st.at(b, 4))
                        nc.vector.scalar_tensor_tensor(out=slot_f[:], in0=ei[:, p, :], scalar=float(CAP), in1=posc[:], op0=ALU.mult, op1=ALU.add).then_inc(st.sem, 1)
                        dve.wait_ge(st.of(b), st.at(b, 5))
                        nc.vector.tensor_scalar(far[:], kept[:], -FAR, FAR, ALU.mult, ALU.add).then_inc(st.sem, 1)
                        dve.wait_ge(st.of(b), st.at(b, 6))
                        if (b - 2).begun:
                            dve.wait_ge(y["route_stored"].of(b - 2), y["route_stored"].at(b - 2))
                        if (b - 2).begun:
                            dve.wait_ge(y["scattered"].of(b - 2), y["scattered"].at(b - 2))
                        dve.wait_ge(y["den_done"].of(b), y["den_done"].at(b))
                        nc.vector.tensor_copy(slot_g[:, p, :], slot_f[:]).then_inc(st.sem, 1)
                        dve.wait_ge(st.of(b), st.at(b, 7))
                        nc.vector.tensor_tensor(slot_s[:, p, :], slot_f[:], far[:], ALU.add).then_inc(st.sem, 1)
                        dve.wait_ge(st.of(b), st.at(b, 8))
                        nc.vector.reciprocal(p8[:], den8[:, p, :]).then_inc(st.sem, 1)
                        dve.wait_ge(st.of(b), st.at(b, 9))
                        nc.vector.scalar_tensor_tensor(out=wgt[:, p, :], in0=p8[:], scalar=g_t[:, 2:3], in1=kept[:], op0=ALU.mult, op1=ALU.mult).then_inc(st.sem, 1)
                        dve.wait_ge(st.of(b), st.at(b, 10))
                    b = s - 3
                    if n == 0 and b.within(B):
                        p = b.parity
                        dve.wait_ge(y["lg_done"].of(b), y["lg_done"].at(b))
                        if (b - 2).begun:
                            dve.wait_ge(y["den_done"].of(b - 2), y["den_done"].at(b - 2))
                        nc.vector.tensor_copy(lg[:, p, :], b7[:, 256:256 + E0]).then_inc(y["lg_read"].sem, 1)
                        dve.wait_ge(y["lg_read"].of(b), y["lg_read"].at(b))
                        if not b.known:
                            carrier()
                        nc.vector.max(top[:], lg[:, p, :]).then_inc(y["top_done"].sem, 1)
                        dve.wait_ge(y["top_done"].of(b), y["top_done"].at(b, 1))
                        nc.vector.tensor_scalar(ntop[:, p, :], top[:, 0:1], -1.0, None, ALU.mult).then_inc(y["top_done"].sem, 1)
                        nc.vector.max_index(topi[:], top[:], lg[:, p, :]).then_inc(y["top_done"].sem, 1)
                        dve.wait_ge(y["top_done"].of(b), y["top_done"].at(b, 3))
                        nc.vector.tensor_copy(ei[:, p, :], topi[:, 0:1]).then_inc(y["top_done"].sem, 1)
                        dve.wait_ge(y["top_done"].of(b), y["top_done"].at(b, 4))
                        if (b - 2).begun:
                            dve.wait_ge(y["cum_done"].of(b - 2), y["cum_done"].at(b - 2))
                        nc.vector.tensor_scalar(onehot[:, p, :], iota_e, ei[:, p, 0:1], None, ALU.is_equal).then_inc(y["top_done"].sem, 1)

                run_steps(dve, B, LEAD, TAIL, WARM, step)
                if n == 0:
                    def split_weights(e):
                        dve.wait_ge(z["w_came"].of(e), z["w_came"].at(e))
                        dve.wait_ge(z["wh_done"].of(e), z["wh_done"].at(e))
                        if At(e.pair, 3 * (e.off - 1) - 1, 6).begun:
                            dve.wait_ge(z["down_done"].of(At(e.pair, 3 * (e.off - 1) - 1, 6)), z["down_done"].at(At(e.pair, 3 * (e.off - 1) - 1, 6)))
                        nc.vector.tensor_tensor(w_lo[:, e.parity], w_raw[:], w_hi[:, e.parity], ALU.subtract).then_inc(z["wl_done"].sem, 1)

                    def turned(g):
                        for c in range(C):
                            dve.wait_ge(z["xg_hi_done"].of(g), z["xg_hi_done"].at(g, c + 1))
                            if c == 0:
                                if (g - 2).begun:
                                    dve.wait_ge(z["up_done"].of(g - 2), z["up_done"].at(g - 2))
                            nc.vector.tensor_tensor(xgt_lo[:, g.parity, c, :], ps[:, 6 + c, 0:G], xgt_hi[:, g.parity, c, :],
                                                    ALU.subtract).then_inc(z["xg_lo_done"].sem, 1)

                    split_weights(At(0, 0))
                    turned(At(0, 0))

                    def estep(e, g, t):
                        for fc in range(FC):
                            dve.wait_ge(z["hid_done"].of(g), z["hid_done"].at(g, fc + 1))
                            if fc == 0:
                                if (g - 1).begun:
                                    dve.wait_ge(z["down_done"].of(g - 1), z["down_done"].at(g - 1))
                            nc.vector.tensor_copy(hid_hi[:, fc, :], hid[:, fc % 2, :]).then_inc(z["hid_hi_done"].sem, 1)
                            dve.wait_ge(z["hid_hi_done"].of(g), z["hid_hi_done"].at(g, fc + 1))
                            nc.vector.tensor_tensor(hid_lo[:, fc, :], hid[:, fc % 2, :], hid_hi[:, fc, :], ALU.subtract)\
                                .then_inc(z["hid_lo_done"].sem, 1)
                        if (g + 1).within(E0 * NG):
                            turned(g + 1)
                        if t == 1 and (e + 1).within(E0):
                            split_weights(e + 1)
                        dve.wait_ge(z["down_done"].of(g), z["down_done"].at(g))
                        if (g - 2).begun:
                            dve.wait_ge(z["eo_stored"].of(g - 2), z["eo_stored"].at(g - 2))
                        for i in range(GT):
                            nc.vector.tensor_tensor(eo[:, g.parity, i, :], ps[:, i, 0:D], b2_in[:, e.parity, :], ALU.add)\
                                .then_inc(z["eo_done"].sem, 1)

                    run_experts(dve, E0, estep)

            dve.wait_ge(s_fw, 16 * 9)
            nc.vector.tensor_scalar(g2_in[:], g2_in[:], g_t[:, 3:4], None, ALU.mult).then_inc(s_fset2, 1)
            nc.vector.tensor_scalar(ones2[:], ident[0:2, :], 0.0, 1.0, ALU.mult, ALU.add).then_inc(s_fset2, 1)
            dve.wait_ge(s_fset, 4)
            nc.vector.tensor_tensor(w1_lo[:], w1f[:], w1_hi[:], ALU.subtract).then_inc(s_fset2, 1)
            nc.vector.tensor_tensor(gw_lo[:], gw_in[:], gw_hi[:], ALU.subtract).then_inc(s_fset2, 1)
            nc.vector.tensor_tensor(b12_lo[:], b12_in[:], b12_hi[:], ALU.subtract).then_inc(s_fset2, 1)
            dve.wait_ge(s_fset2, 5)
            nc.vector.tensor_scalar(b12_lo[:], b12_lo[:], hilo_mask[:, 1:2], None, ALU.mult).then_inc(s_fset2, 1)
            dve.wait_ge(s_fset2, 6)
            nc.vector.scalar_tensor_tensor(out=b12[:].rearrange("p a e n -> p (a e n)"),
                                           in0=b12_hi[:].rearrange("p a e n -> p (a e n)"), scalar=hilo_mask[:, 0:1],
                                           in1=b12_lo[:].rearrange("p a e n -> p (a e n)"),
                                           op0=ALU.mult, op1=ALU.add).then_inc(s_fset2, 1)
            dve.wait_ge(s_fset2, 7)
            dve.wait_ge(y1["x1_stored"].of(At(0, B - 1)), y1["x1_stored"].at(At(0, B - 1)))
            dve.wait_ge(y1["x1_stored"].of(At(0, B - 2)), y1["x1_stored"].at(At(0, B - 2)))
            nc.vector.memset(gpad[:], -3.0e38).then_inc(s_fset2, 1)

            def stats(banks, st, sig, done, b, half):
                dve.wait_ge(done.of(b), done.at(b, half + 1))
                for e in (2 * half, 2 * half + 1):
                    nc.vector.bn_stats(st[:, e, :], ps[:, banks + half, (e % 2) * D:(e % 2 + 1) * D]).then_inc(sig.sem, 1)

            def stats_in_all(st, mv, sig, b):
                dve.wait_ge(sig.of(b), sig.at(b, E1))
                if not b.known:
                    carrier()
                for e in range(E1):
                    nc.vector.bn_aggr(mv[:, e, :], st[:, e, :]).then_inc(sig.sem, 1)

            def fstep(s):
                b = s - 2
                if b.within(B):
                    stats(6, k_st, f["k_stats"], f["down1_done"], b, 0)
                b = s
                if b.within(B):
                    dve.wait_ge(f["x_hi_done"].of(b), f["x_hi_done"].at(b))
                    nc.vector.tensor_tensor(xft_lo[:, b.parity].rearrange("p c k -> p (c k)"), ps[:, 0, 0:D],
                                            xft_hi[:, b.parity].rearrange("p c k -> p (c k)"), ALU.subtract).then_inc(f["x_lo_done"].sem, 1)
                b = s - 2
                if b.within(B):
                    stats(6, k_st, f["k_stats"], f["down1_done"], b, 1)
                    stats_in_all(k_st, k_mv, f["k_stats"], b)
                b = s - 1
                if b.within(B):
                    gm = f["gate_mix"]
                    dve.wait_ge(f["gexp_done"].of(b), f["gexp_done"].at(b))
                    if (b - 2).begun:
                        dve.wait_ge(f["gw_turned"].of(b - 2), f["gw_turned"].at(b - 2))
                    nc.vector.tensor_scalar(gsum[:], gexp[:], 1.0, None, ALU.add).then_inc(gm.sem, 1)
                    dve.wait_ge(gm.of(b), gm.at(b, 1))
                    nc.vector.reciprocal(gw[:, 0:1], gsum[:]).then_inc(gm.sem, 1)
                    dve.wait_ge(gm.of(b), gm.at(b, 2))
                    nc.vector.tensor_tensor(gw[:, 1:2], gexp[:], gw[:, 0:1], ALU.mult).then_inc(gm.sem, 1)
                    nc.vector.tensor_scalar(gwa[:], iota_e[:, 0:E1], gidx[:, 0:1], gw[:, 0:1], ALU.is_equal, ALU.mult).then_inc(gm.sem, 1)
                    dve.wait_ge(gm.of(b), gm.at(b, 3))
                    nc.vector.tensor_scalar(gwb[:], iota_e[:, 0:E1], gidx[:, 1:2], gw[:, 1:2], ALU.is_equal, ALU.mult).then_inc(gm.sem, 1)
                    dve.wait_ge(gm.of(b), gm.at(b, 5))
                    nc.vector.tensor_tensor(gwt[:, b.parity, :], gwa[:], gwb[:], ALU.add).then_inc(gm.sem, 1)
                b = s - 2
                if b.within(B):
                    dve.wait_ge(f["k_rstd"].of(b), f["k_rstd"].at(b))
                    if (b - 1).begun:
                        dve.wait_ge(f["u_done"].of(b - 1), f["u_done"].at(b - 1))
                    nc.vector.tensor_tensor(k_rw[:], k_rs[:, 1, :], gwt[:, b.parity, :], ALU.mult).then_inc(f["k_steps"].sem, 1)
                    dve.wait_ge(f["k_steps"].of(b), f["k_steps"].at(b, 1))
                    nc.vector.scalar_tensor_tensor(out=k_nm[:], in0=k_mv[:, :, 0], scalar=-1.0, in1=k_rw[:],
                                                   op0=ALU.mult, op1=ALU.mult).then_inc(f["k_steps"].sem, 1)
                b = s
                if b.within(B):
                    stats(2, h_st, f["h_stats"], f["up1_done"], b, 0)
                    stats(2, h_st, f["h_stats"], f["up1_done"], b, 1)
                    stats_in_all(h_st, h_mv, f["h_stats"], b)
                b = s + 1
                if b.within(B):
                    dve.wait_ge(f["x3_came"].of(b), f["x3_came"].at(b))
                    nc.vector.bn_stats(fst[:], x3[:, b.off % 4, :]).then_inc(f["st"].sem, 1)
                    dve.wait_ge(f["st"].of(b), f["st"].at(b, 1))
                    if not b.known:
                        carrier()
                    nc.vector.bn_aggr(fmv[:], fst[:]).then_inc(f["st"].sem, 1)
                b = s - 3
                if b.within(B):
                    mx = f["mix"]
                    dve.wait_ge(f["summed"].of(b), f["summed"].at(b))
                    if (b - 2).begun:
                        dve.wait_ge(f["x4_stored"].of(b - 2), f["x4_stored"].at(b - 2))
                    nc.vector.tensor_tensor(x4[:, b.parity, :], mix2[:], u2t[:], ALU.add).then_inc(mx.sem, 1)
                b = s
                if b.within(B):
                    gs = f["gate_steps"]
                    dve.wait_ge(f["gates_done"].of(b), f["gates_done"].at(b))
                    nc.vector.tensor_tensor(gpad[:, b.parity, 0:E1], ps[:, 0, 256:256 + E1], gb_in[:], ALU.add).then_inc(f["gates_read"].sem, 1)
                    dve.wait_ge(f["gates_read"].of(b), f["gates_read"].at(b))
                    if not b.known:
                        carrier()
                    nc.vector.max(gtop[:], gpad[:, b.parity, :]).then_inc(gs.sem, 1)
                    dve.wait_ge(gs.of(b), gs.at(b, 1))
                    if not b.known:
                        carrier()
                    nc.vector.max_index(gtopi[:], gtop[:], gpad[:, b.parity, :]).then_inc(gs.sem, 1)
                    dve.wait_ge(gs.of(b), gs.at(b, 2))
                    nc.vector.tensor_copy(gidx[:], gtopi[:, 0:2]).then_inc(gs.sem, 1)
                    if (b - 1).begun:
                        dve.wait_ge(f["gexp_done"].of(b - 1), f["gexp_done"].at(b - 1))
                    nc.vector.tensor_tensor(gdiff[:], gtop[:, 1:2], gtop[:, 0:1], ALU.subtract).then_inc(gs.sem, 1)
                    dve.wait_ge(f["h_rstd"].of(b), f["h_rstd"].at(b))
                    if (b - 1).begun:
                        dve.wait_ge(f["z_act"].of(b - 1), f["z_act"].at(b - 1))
                    nc.vector.scalar_tensor_tensor(out=h_nm[:], in0=h_mv[:, :, 0], scalar=-1.0, in1=h_rs[:, 1, :],
                                                   op0=ALU.mult, op1=ALU.mult).then_inc(f["h_nm_done"].sem, 1)
                    if (b - 2).begun:
                        dve.wait_ge(f["z_turned"].of(b - 2), f["z_turned"].at(b - 2))
                    for e in range(2, E1):
                        nc.vector.tensor_scalar(z1[:, b.parity, e, :], ps[:, 3, (e - 2) * D:(e - 1) * D], h_mv[:, e, 0:1],
                                                h_rs[:, 1, e:e + 1], ALU.subtract, ALU.mult).then_inc(f["z_dve"].sem, 1)
                b = s
                if b.within(B):
                    if (b - 4).begun:
                        dve.wait_ge(f["mix"].of(b - 4), f["mix"].at(b - 4))
                    nc.vector.scalar_tensor_tensor(out=mix1[:, b.off % 4, :], in0=xf[:, b.off % 4, :], scalar=g_t[:, 3:4],
                                                   in1=x3[:, b.off % 4, :], op0=ALU.mult, op1=ALU.add)\
                        .then_inc(f["base_done"].sem, 1)
                b = s + 1
                if b.within(B):
                    dve.wait_ge(f["rstd"].of(b), f["rstd"].at(b))
                    nc.vector.tensor_scalar(xf[:, b.off % 4, :], x3[:, b.off % 4, :], fmv[:, 0:1], frs[:, 1:2], ALU.subtract, ALU.mult)\
                        .then_inc(f["xf_done"].sem, 1)

            run_steps(dve, B, 2, 3, 8, fstep, 4)


def constants():
    import numpy as np
    c = np.zeros((128, 278), np.float32)
    p = np.arange(128)
    c[:, 0:128] = np.eye(128)
    c[:, 128] = (p // 16) % 2 == 0
    c[:, 129] = (p // 16) % 2 == 1
    for t in range(4):
        c[:, 130 + t] = (p % 4 == t) & (p < 16)
        c[:, 142 + t] = (p // 4 == t)
    c[:, 134:142] = np.arange(8)
    c[:, 146:274] = p[:, None] <= p[None, :]
    c[0, 274] = 1
    c[1, 275] = 1
    c[:, 276] = -0.5
    c[:, 277] = LN_EPS
    return c


def _lay_out(i):
    import numpy as np
    B = i["x"].shape[0]
    a = {k: np.asarray(v) for k, v in i.items()}

    def rows(w):
        return w.reshape(-1, 128, w.shape[-1]).transpose(1, 0, 2)

    def by_score_order(w):
        return w.reshape(2, 4, 2, 16, -1).transpose(1, 0, 2, 3, 4).reshape(w.shape)

    w0 = a["L0_xattn_W_qkv"]
    q0, k0, v0 = w0[:, 0:256], w0[:, 256:512], w0[:, 512:768]
    d = {
        "x": a["x"], "ctx_in": a["ctx_1024"], "consts": constants(),
        "gates": np.broadcast_to(np.concatenate([a["g_xattn"], a["g_ffn"]])[None, :], (128, 4)),
        "wq": np.stack([rows(q0), rows(a["L1_xattn_wq"].T)]),
        "wk": np.stack([rows(k0), rows(a["L1_xattn_wk"].T)]),
        "wv": np.stack([rows(v0), rows(a["L1_xattn_wv"].T)]),
        "wp": np.stack([rows(by_score_order(a["L0_xattn_W_proj"])), rows(by_score_order(a["L1_xattn_wo"].T))]),
        "b_proj": np.broadcast_to(a["L0_xattn_b_proj"][None, :], (128, 256)),
        "router": rows(a["L0_ffn_router_w"].T),
        "w1_0": a["L0_ffn_w1"].reshape(8, 2, 128, 1024).transpose(0, 2, 1, 3),
        "b1_0": a["L0_ffn_b1"].reshape(8, 8, 128).transpose(0, 2, 1),
        "w2_0": a["L0_ffn_w2"].reshape(8, 8, 128, 256).transpose(0, 2, 1, 3),
        "b2_0": np.broadcast_to(a["L0_ffn_b2"][:, None, :], (8, 128, 256)),
        "gate_w": rows(a["L1_ffn_gate_W"]),
        "gate_b": np.broadcast_to(a["L1_ffn_gate_b"][None, :], (128, 4)),
        "w1_1": a["L1_ffn_W1"].reshape(4, 2, 128, 256).transpose(2, 0, 1, 3),
        "b12_1": np.broadcast_to(np.stack([a["L1_ffn_b1"], a["L1_ffn_b2"]])[None], (2, 2, 4, 256)),
        "g1_1": a["L1_ffn_g1"].reshape(4, 2, 128).transpose(2, 0, 1),
        "be1_1": a["L1_ffn_be1"].reshape(4, 2, 128).transpose(2, 0, 1),
        "w2_1": a["L1_ffn_W2"].reshape(4, 2, 128, 256).transpose(2, 0, 1, 3),
        "g2_1": np.broadcast_to(a["L1_ffn_g2"][None], (128, 4, 256)), "be2_1": a["L1_ffn_be2"],
    }
    return {k: np.ascontiguousarray(v) for k, v in d.items()}


def kernel(**inputs):
    import numpy as _np
    import concourse.bacc as _bacc
    from concourse import mybir as _mybir
    from concourse.bass_utils import run_bass_kernel_spmd as _run

    nc = _bacc.Bacc("TRN2", target_bir_lowering=False, num_devices=1)
    arrays, args = {}, {}
    for name, a in _lay_out(inputs).items():
        arrays[f"in_{name}_dram"] = a
        args[name] = nc.dram_tensor(f"in_{name}_dram", a.shape, _mybir.dt.from_np(a.dtype), kind="ExternalInput").ap()
    shape = _np.asarray(inputs["x"]).shape
    out = nc.dram_tensor("out_0_dram", shape, _mybir.dt.float32, kind="ExternalOutput").ap()
    flamingo_gated(nc, out=out, **args)
    r = _run(nc, [arrays], core_ids=[0])
    return r.results[0]["out_0_dram"]
```
